# Optimizing a Trainium2 kernel written in Bass

```python
import numpy as np
import jax
import jax.numpy as jnp

def _softmax(x, axis=-1):
    return jax.nn.softmax(x, axis=axis)

def _gelu(x):
    return jax.nn.gelu(x, approximate=True)

def _silu(x):
    return jax.nn.silu(x)

def _sigmoid(x):
    return jax.nn.sigmoid(x)

def _layernorm(x, axis=-1, eps=1e-05):
    m = jnp.mean(x, axis=axis, keepdims=True)
    v = jnp.var(x, axis=axis, keepdims=True)
    return (x - m) / jnp.sqrt(v + eps)

def _scatter_add(tgt, idx, src, axis=0):
    return tgt.at[idx].add(src)

def _segment_sum(src, seg, n):
    return jax.ops.segment_sum(src, seg, n)
kernel_name = 'mk_seq_preln_d1_jaxref_r8_1b57e4'

def setup_inputs(seed: int=0):
    np.random.seed(seed)
    _w = jnp.asarray

    def _L0_attn_setup():
        import jax, jax.numpy as jnp
        import numpy as np
        B, T, C, H = (4, 128, 128, 16)
        D = C // H

        def _expmap0_split(u):
            mink = -u[..., :1] ** 2 + jnp.sum(u[..., 1:] ** 2, axis=-1, keepdims=True)
            nomin = jnp.sqrt(jnp.maximum(mink, 1e-08))
            time = jnp.cosh(nomin)
            space = jnp.sinh(nomin) * u[..., 1:] / nomin
            return (time, space)
        key = jax.random.key(seed)
        ks = jax.random.split(key, 6)
        s = 1.0 / np.sqrt(C)
        return {'x': jax.random.normal(ks[0], (B, T, C), jnp.float32), 'W_qkv': jax.random.normal(ks[1], (C, 3 * C), jnp.float32) * s, 'b_qkv': jnp.zeros((3 * C,), jnp.float32), 'W_out': jax.random.normal(ks[2], (C, C), jnp.float32) * s, 'b_out': jnp.zeros((C,), jnp.float32), 'w_sur': jax.random.normal(ks[3], (C,), jnp.float32) * s, 'b_sur': jnp.zeros((), jnp.float32), 'threshold': jnp.float32(0.5)}
    _L0_attn_in = _L0_attn_setup()

    def _L0_ffn_setup():
        import jax, jax.numpy as jnp
        import numpy as np
        DIM = 128
        HIDDEN = 384
        SCALE = 1.0 / 127.0

        def _dequant(w_int, dtype):
            return w_int.astype(dtype) * jnp.asarray(SCALE, dtype)
        key = jax.random.key(seed)
        k_x, k_g, k_u, k_d = jax.random.split(key, 4)
        x = jax.random.normal(k_x, (4, 256, DIM), dtype=jnp.float32)
        w_gate = jax.random.randint(k_g, (HIDDEN, DIM), -127, 128, dtype=jnp.int32)
        w_up = jax.random.randint(k_u, (HIDDEN, DIM), -127, 128, dtype=jnp.int32)
        w_down = jax.random.randint(k_d, (DIM, HIDDEN), -127, 128, dtype=jnp.int32)
        return {'x': x, 'w_gate': w_gate, 'w_up': w_up, 'w_down': w_down}
    _L0_ffn_in = _L0_ffn_setup()
    _d = {'L0_attn_x': _L0_attn_in['x'], 'L0_attn_W_qkv': _L0_attn_in['W_qkv'], 'L0_attn_b_qkv': _L0_attn_in['b_qkv'], 'L0_attn_W_out': _L0_attn_in['W_out'], 'L0_attn_b_out': _L0_attn_in['b_out'], 'L0_attn_w_sur': _L0_attn_in['w_sur'], 'L0_attn_b_sur': _L0_attn_in['b_sur'], 'L0_attn_threshold': _L0_attn_in['threshold'], 'L0_ffn_w_gate': _L0_ffn_in['w_gate'], 'L0_ffn_w_up': _L0_ffn_in['w_up'], 'L0_ffn_w_down': _L0_ffn_in['w_down']}
    _x0 = _d['L0_attn_x']
    _d['L0_attn_x'] = jax.random.normal(jax.random.fold_in(jax.random.key(seed), 1), (2, 1024, 128), dtype=_x0.dtype)
    del _x0
    return _d

def reference(L0_attn_x, L0_attn_W_qkv, L0_attn_b_qkv, L0_attn_W_out, L0_attn_b_out, L0_attn_w_sur, L0_attn_b_sur, L0_attn_threshold, L0_ffn_w_gate, L0_ffn_w_up, L0_ffn_w_down):

    def _L0_attn_ref(x, W_qkv, b_qkv, W_out, b_out, w_sur, b_sur, threshold):
        import jax, jax.numpy as jnp
        import numpy as np
        B, T, C, H = (4, 128, 128, 16)
        D = C // H

        def _expmap0_split(u):
            mink = -u[..., :1] ** 2 + jnp.sum(u[..., 1:] ** 2, axis=-1, keepdims=True)
            nomin = jnp.sqrt(jnp.maximum(mink, 1e-08))
            time = jnp.cosh(nomin)
            space = jnp.sinh(nomin) * u[..., 1:] / nomin
            return (time, space)
        Bx, Tx, Cx = x.shape
        importance = jax.nn.sigmoid(jnp.einsum('btc,c->bt', x, w_sur) + b_sur)
        spikes = (importance > threshold).astype(x.dtype)
        spike_mask = spikes[:, None, :, None]
        qkv = x @ W_qkv + b_qkv
        qkv = qkv.reshape(Bx, Tx, 3, H, D).transpose(2, 0, 3, 1, 4)
        q, k, v = (qkv[0], qkv[1], qkv[2])
        tq, sq = _expmap0_split(q)
        tk, sk = _expmap0_split(k)
        neg_inner = jnp.einsum('bhie,bhje->bhij', tq, tk) - jnp.einsum('bhid,bhjd->bhij', sq, sk)
        dist = jnp.arccosh(jnp.maximum(neg_inner, 1.0 + 1e-07))
        scores = -dist ** 2 / np.sqrt(D)
        causal = jnp.tril(jnp.ones((Tx, Tx), dtype=bool))
        scores = jnp.where(causal[None, None], scores, -jnp.inf)
        attn = jax.nn.softmax(scores, axis=-1) * spike_mask
        y = jnp.einsum('bhij,bhjd->bhid', attn, v)
        y = y.transpose(0, 2, 1, 3).reshape(Bx, Tx, Cx)
        return y @ W_out + b_out

    def _L0_ffn_ref(x, w_gate, w_up, w_down):
        import jax, jax.numpy as jnp
        import numpy as np
        DIM = 128
        HIDDEN = 384
        SCALE = 1.0 / 127.0

        def _dequant(w_int, dtype):
            return w_int.astype(dtype) * jnp.asarray(SCALE, dtype)
        wg = _dequant(w_gate, x.dtype)
        wu = _dequant(w_up, x.dtype)
        wd = _dequant(w_down, x.dtype)
        gate = jnp.einsum('bsd,hd->bsh', x, wg)
        up = jnp.einsum('bsd,hd->bsh', x, wu)
        h = jax.nn.silu(gate) * up
        return jnp.einsum('bsh,dh->bsd', h, wd)
    x = L0_attn_x
    x = x + _L0_attn_ref(_layernorm(x, axis=-1), L0_attn_W_qkv, L0_attn_b_qkv, L0_attn_W_out, L0_attn_b_out, L0_attn_w_sur, L0_attn_b_sur, L0_attn_threshold)
    x = x + _L0_ffn_ref(_layernorm(x, axis=-1), L0_ffn_w_gate, L0_ffn_w_up, L0_ffn_w_down)
    return x

_drawn_inputs = setup_inputs


def setup_inputs(seed=0):
    import zlib

    import numpy as np

    out = dict(_drawn_inputs(seed))
    spreads = {'L0_attn_b_qkv': (0.0, 0.1), 'L0_attn_b_out': (0.0, 0.1)}
    factors = {}
    for name, (base, spread) in spreads.items():
        noise = np.random.default_rng([zlib.crc32(name.encode()), seed]).standard_normal(out[name].shape)
        drawn = base * np.exp(spread * noise) if base else spread * noise
        out[name] = jnp.asarray(drawn.astype(out[name].dtype))
    for name, factor in factors.items():
        out[name] = (out[name] * factor).astype(out[name].dtype)
    return out
```

```python
import numpy as np
import concourse.bass as bass
from concourse import mybir
from contextlib import ExitStack

fp32 = mybir.dt.float32
bf16 = mybir.dt.bfloat16
i32 = mybir.dt.int32
ALU = mybir.AluOpType
ACT = mybir.ActivationFunctionType
AX = mybir.AxisListType

P = 128
B, T, C, H, HID = 2, 1024, 128, 16, 384
D = C // H
NT = T // P
TT = B * NT
U = 4
G = B * H // U
QUADS = H // U
BANK = 512
OFF = [t * (t + 1) // 2 * P for t in range(NT + 1)]
FU = OFF[NT]
FB = FU + NT
VW = D + 1
PARTS = 3
ROWS = 64
NTB, NPT = 2, 4
CH = [(c, jt) for c in range(2) for jt in range(4 * c + 4)]
NCH = len(CH)
NSTK = 11 * 16
EPS_LN = 1e-5
ONE_EPS = float(np.float32(1.0 + 1e-7))
MASKED = 1e35
SIGMA = 2.0 ** 0.5
NW = 3 * C + 1
HB = HID // P
COSH = [1 / 2, 1 / 24, 1 / 720, 1 / 40320, 1 / 3628800]
SINH = [1 / 6, 1 / 120, 1 / 5040, 1 / 362880, 1 / 39916800]


def layer(nc, x, w_qkv, b_qkv, w_out, b_out, w_sur, b_sur, threshold, w_gate, w_up, w_down, out):
    with ExitStack() as ctx:
        def sb(name, shape, dt=fp32):
            return ctx.enter_context(nc.sbuf_tensor(name, shape, dt))

        def sem(name):
            return ctx.enter_context(nc.semaphore(name))

        parts = nc.dram_tensor("qk_parts", [2, B * H, PARTS * D, T], bf16, kind="Internal").ap()

        Z = sb("Z", [P, U, FB])
        X = sb("X", [P, 2, FB])
        xres = sb("xres", [P, TT, C])
        Y = sb("Y", [P, TT, C])
        V9 = sb("V9", [P, G, NT * U * VW])
        Vg = sb("Vg", [P, NT, U, VW])
        PT = sb("PT", [P, NPT, BANK])
        Qs = sb("Qs", [P, 2, T], bf16)
        Ks = sb("Ks", [P, 2, T], bf16)
        Dg = sb("Dg", [P, 2, NT, P], bf16)
        yS = sb("yS", [P, T])
        W = sb("W", [P, NW])
        Wb = sb("Wb", [P, NW])
        Wo = sb("Wo", [P, C])
        bo = sb("bo", [P, C])
        thr = sb("thr", [P, 1])
        wint = sb("wint", [P, 3 * HB, P], i32)
        wT = sb("wT", [P, 3 * HB, P])
        ident = sb("ident", [P, P])
        identb = sb("identb", [P, P], bf16)
        nident = sb("nident", [P, P])
        onesb = sb("onesb", [P, P], bf16)
        maskb = sb("maskb", [P, P], bf16)
        epsln = sb("epsln", [P, 1])
        mhalf = sb("mhalf", [P, 1])
        phalf = sb("phalf", [P, 1])
        st6 = sb("st6", [P, TT, 6])
        mv = sb("mv", [P, TT, 2])
        sd = sb("sd", [P, TT])
        rstd = sb("rstd", [P, TT])
        sur = sb("sur", [P, TT])
        sg = sb("sg", [P, TT])
        spike = sb("spike", [P, G, NT])
        den = sb("den", [P, NT, U])
        PS = ctx.enter_context(nc.psum_tensor("PS", [P, 8, BANK], fp32))

        uq = X[:, 0, 0:TT * 2 * C].rearrange("p (t c) -> p t c", t=TT)
        usq = X[:, 1, 0:TT * 2 * C]
        wf = Y[:].rearrange("p t c -> p (t c)")[:, 0:3 * HB * P]
        xn = X[:, 1, 0:TT * C].rearrange("p (t c) -> p t c", t=TT)
        xnT = Z[:, 0, 0:TT * P]
        split = Z[:, 2:4, 0:PARTS * B * T // 2].bitcast(bf16).rearrange("p s (n t) -> p s n t", n=PARTS)
        small = [Z[:, 0, TT * P + 512 * i:TT * P + 512 * (i + 1)] for i in range(5)] + \
                [Z[:, 1, 512 * i:512 * (i + 1)] for i in range(9)]
        mk, mc, n0, rn, n2, ex, ei, ch, sh, co, p1, p2, cs, tmp = small
        msk = tmp.bitcast(i32)
        rem = PT
        x1 = Z[:, 0, 0:TT * C].rearrange("p (t c) -> p t c", t=TT)
        yT = Z[:, 1, 0:TT * P]
        xn2 = Z[:, 2, 0:TT * C].rearrange("p (t c) -> p t c", t=TT)
        xn2T = Z[:, 3, 0:TT * P]
        sil = X[:, 0, 0:2 * BANK].rearrange("p (n t) -> p n t", n=2)
        hT = X[:, 1, 0:2 * HB * BANK].rearrange("p (n a t) -> p n a t", n=2, a=HB)
        res = X[:, 0, 2 * BANK:6 * BANK].rearrange("p (n t c) -> p n t c", n=4, t=4)

        x_in = [sem(f"x_in{n}") for n in range(4)]
        w_in, wo_in, wi_in = sem("w_in"), sem("wo_in"), sem("wi_in")
        consts, wf_ready = sem("consts"), sem("wf_ready")
        dve_s, pool_s = sem("dve_s"), sem("pool_s")
        var_ready, sd_ready, xn_ready, tr_ready, tr_copied = (sem(n) for n in (
            "var_ready", "sd_ready", "xn_ready", "tr_ready", "tr_copied"))
        qkv_ready, qkv_used, usq_ready, mk_ready, root_ready, n2_ready, ex_ready, hat_ready = (sem(n) for n in (
            "qkv_ready", "qkv_used", "usq_ready", "mk_ready", "root_ready", "n2_ready", "ex_ready", "hat_ready"))
        sur_ready, sg_ready = sem("sur_ready"), sem("sg_ready")
        hatT_ready, h1_ready, r1_ready, h2_ready, h3_ready = (sem(n) for n in (
            "hatT_ready", "h1_ready", "r1_ready", "h2_ready", "h3_ready"))
        stored = sem("stored")
        stacks = [sem(f"stacks{u}") for u in range(U)]
        z_ready, z_used, roots_ready, sum_ready, log_ready, sq_ready, diag_ready, v_ready = (sem(n) for n in (
            "z_ready", "z_used", "roots_ready", "sum_ready", "log_ready", "sq_ready", "diag_ready", "v_ready"))
        t_ready, p_ready, pv_done, o_saved, yT_ready, den_step, y_norm = (sem(n) for n in (
            "t_ready", "p_ready", "pv_done", "o_saved", "yT_ready", "den_step", "y_norm"))
        e_yT, e_yTc, e_at, e_x1, e_var, e_sd, e_xn, e_xT, e_xTc, e_gu, e_sil, e_h, e_dn, e_res, e_out = (
            sem("e_" + n) for n in ("yT", "yTc", "at", "x1", "var", "sd", "xn", "xT", "xTc", "gu", "sil", "h",
                                    "dn", "res", "out"))

        block = ctx.enter_context(nc.Block())

        @block.sync
        def _(sp):
            xt = x.rearrange("b (t p) c -> p (b t) c", p=P)
            for n in range(4):
                sp.dma_start(xres[:, 4 * n:4 * n + 4, :], xt[:, 4 * n:4 * n + 4, :]).then_inc(x_in[n], 16)
            sp.dma_start(wint[:, 0:HB, :], w_gate.rearrange("(a p) d -> p a d", p=P)).then_inc(wi_in, 16)
            sp.dma_start(wint[:, HB:2 * HB, :], w_up.rearrange("(a p) d -> p a d", p=P)).then_inc(wi_in, 16)
            sp.dma_start(wint[:, 2 * HB:3 * HB, :], w_down.rearrange("d (a h) -> d a h", a=HB)).then_inc(wi_in, 16)

            for b in range(B):
                sp.wait_ge(h3_ready, 4 * (b + 1))
                for s in range(2):
                    for n in range(PARTS):
                        sp.dma_start(
                            parts[s, b * H:(b + 1) * H, n * D:(n + 1) * D, :],
                            split[:, s, n, b * T:(b + 1) * T]).then_inc(stored, 16)

            def load_stacks(n, u):
                r0, pr = ROWS * (u % 2), u // 2
                for first, reps, part in ((0, 3, 0), (24, 3, 1), (48, 2, 2)):
                    src = parts[0, bass.ds(n, 1), part * D:(part + 1) * D, :].rearrange("o d t -> (o d) t")
                    for rep in range(reps):
                        a = r0 + first + rep * D
                        sp.dma_start(Qs[a:a + D, pr, :], src).then_inc(stacks[u], 16)
                for first, rows in ((0, 24), (24, 24), (48, 16)):
                    src = parts[1, bass.ds(n, 1), 0:rows, :].rearrange("o d t -> (o d) t")
                    sp.dma_start(Ks[r0 + first:r0 + first + rows, pr, :], src).then_inc(stacks[u], 16)

            sp.wait_ge(stored, 16 * 2 * PARTS * B)
            for u in range(U):
                load_stacks(u, u)
            with sp.Fori(0, G - 1) as g:
                for u in range(U):
                    sp.wait_ge(z_ready, g * (U * NT) + (u + 1) * NT)
                    load_stacks(g * U + (U + u), u)

            ot = out.rearrange("b (t p) c -> p (b t) c", p=P)
            for n in range(4):
                sp.wait_ge(e_res, n + 1)
                sp.dma_start(ot[:, 4 * n:4 * n + 4, :], res[:, n]).then_inc(e_out, 16)
            sp.wait_ge(e_out, 64)

        @block.gpsimd
        def _(pool):
            nc.gpsimd.memset(ident[:], 0.0).then_inc(pool_s, 1)
            nc.gpsimd.memset(maskb[:], 0.0).then_inc(pool_s, 1)
            nc.gpsimd.memset(V9[:], 1.0).then_inc(consts, 1)
            nc.gpsimd.memset(onesb[:], 1.0).then_inc(consts, 1)
            pool.wait_ge(pool_s, 2)
            nc.gpsimd.affine_select(out=ident[:], in_=ident[:], compare_op=ALU.not_equal, fill=1.0, base=0,
                                    pattern=[[-1, P]], channel_multiplier=1).then_inc(pool_s, 1)
            nc.gpsimd.affine_select(out=maskb[:], in_=maskb[:], compare_op=ALU.is_ge, fill=MASKED, base=0,
                                    pattern=[[-1, P]], channel_multiplier=1).then_inc(consts, 1)
            pool.wait_ge(pool_s, 3)
            nc.gpsimd.tensor_copy(identb[:], ident[:]).then_inc(consts, 1)
            nc.gpsimd.tensor_scalar(nident[:], ident[:], -1.0, 0.0, ALU.mult, ALU.add).then_inc(consts, 1)
            pool.wait_ge(wi_in, 48)
            nc.gpsimd.tensor_scalar(wf, wint[:].rearrange("p a d -> p (a d)"),
                                    float(np.float32(1.0 / 127.0)), 0.0, ALU.mult, ALU.add).then_inc(wf_ready, 1)

            with pool.Fori(0, G) as g:
                pool.wait_ge(y_norm, g + 1)
                pool.wait_ge(qkv_used, TT)
                nc.gpsimd.tensor_copy(Vg[:].rearrange("p t u w -> p (t u w)"),
                                      V9[:].rearrange("p g w -> p (g w)")[:, bass.ds(g * (NT * U * VW), NT * U * VW)]
                                      ).then_inc(v_ready, 1)
                for u in range(U):
                    pool.wait_ge(sq_ready, g * U + (u + 1))
                    if u >= 2:
                        pool.wait_ge(t_ready, g * (U * NCH) + NCH * (u - 1))
                    nc.gpsimd.tensor_tensor(
                        Dg[:, u % 2], nident[:].unsqueeze(1).to_broadcast([P, NT, P]),
                        Z[:, u, FU:FB].unsqueeze(2).to_broadcast([P, NT, P]), ALU.mult).then_inc(diag_ready, 1)

        @block.scalar
        def _(act):
            act.dma_start(W[:, 0:3 * C], w_qkv).then_inc(w_in, 16)
            act.dma_start(W[:, 3 * C:NW], w_sur.unsqueeze(1)).then_inc(w_in, 16)
            act.dma_start(Wb[:, 0:3 * C], b_qkv.partition_broadcast(P)).then_inc(w_in, 16)
            act.dma_start(Wb[:, 3 * C:NW], b_sur.partition_broadcast(P)).then_inc(w_in, 16)
            act.dma_start(thr[:], threshold.partition_broadcast(P)).then_inc(w_in, 16)
            act.dma_start(Wo[:], w_out).then_inc(wo_in, 16)
            act.dma_start(bo[:], b_out.partition_broadcast(P)).then_inc(wo_in, 16)

            act.wait_ge(var_ready, 1)
            nc.scalar.activation(sd[:], mv[:, :, 1], ACT.Sqrt, bias=epsln[:]).then_inc(sd_ready, 1)
            for n in range(4):
                act.wait_ge(tr_ready, n + 1)
                nc.scalar.copy(xnT[:, n * BANK:(n + 1) * BANK], PS[:, n % 2, :]).then_inc(tr_copied, 1)
            for n in range(3):
                act.wait_ge(tr_ready, n + 5)
                nc.scalar.copy(wT[:, HB * n:HB * (n + 1), :].rearrange("p a d -> p (a d)"),
                               PS[:, n % 2, 0:HID]).then_inc(tr_copied, 1)
            for b in range(B):
                act.wait_ge(qkv_used, NT * (b + 1))
                w = NT * 2 * C
                nc.scalar.activation(usq[:, b * w:(b + 1) * w],
                                     uq[:, b * NT:(b + 1) * NT, :].rearrange("p t c -> p (t c)"),
                                     ACT.Square).then_inc(usq_ready, 1)
            act.wait_ge(mk_ready, 1)
            nc.scalar.activation(n0, mk, ACT.Sqrt).then_inc(root_ready, 1)
            act.wait_ge(n2_ready, 1)
            nc.scalar.activation(ex, n2, ACT.Exp, scale=0.5).then_inc(ex_ready, 1)
            act.wait_ge(sur_ready, 1)
            nc.scalar.activation(sg[:], sur[:], ACT.Exp, scale=-1.0).then_inc(sg_ready, 1)
            for k in range(8):
                n, s = k // 2, k % 2
                act.wait_ge(hatT_ready, k + 1)
                nc.scalar.copy(split[:, s, 0, n * BANK:(n + 1) * BANK], PS[:, k % 4, :]).then_inc(h1_ready, 1)
                act.wait_ge(r1_ready, k + 1)
                nc.scalar.copy(split[:, s, 1, n * BANK:(n + 1) * BANK], rem[:, k % 2, :]).then_inc(h2_ready, 1)

            def log(g, u):
                act.wait_ge(sum_ready, g * U + (u + 1))
                nc.scalar.activation(Z[:, u, :], Z[:, u, :], ACT.Ln).then_inc(log_ready, 1)

            def exps(g, u):
                for k, (c, jt) in enumerate(CH):
                    n = u * NCH + k
                    w = BANK - max(jt - 4 * c, 0) * P
                    act.wait_ge(t_ready, g * (U * NCH) + (n + 1))
                    if n >= NPT:
                        act.wait_ge(pv_done, g * (U * NCH) + (n + 1 - NPT))
                    nc.scalar.activation(PT[:, n % NPT, BANK - w:BANK], PS[:, 4 + n % NTB, BANK - w:BANK], ACT.Exp,
                                         scale=-SIGMA).then_inc(p_ready, 1)

            with act.Fori(0, G) as g:
                for u in range(U):
                    act.wait_ge(z_used, g * (U * NT) + (u + 1) * NT)
                    if u >= 2:
                        act.wait_ge(sum_ready, g * U + (u - 1))
                    nc.scalar.activation(X[:, u % 2, :], Z[:, u, :], ACT.Sqrt, scale=0.5, bias=mhalf[:])
                    nc.scalar.activation(Z[:, u, :], Z[:, u, :], ACT.Sqrt, scale=0.5, bias=phalf[:]
                                         ).then_inc(roots_ready, 1)
                log(g, 0)
                log(g, 1)
                log(g, 2)
                exps(g, 0)
                log(g, 3)
                exps(g, 1)
                exps(g, 2)
                exps(g, 3)

            for n in range(4):
                act.wait_ge(e_yT, n + 1)
                nc.scalar.copy(yT[:, n * BANK:(n + 1) * BANK], PS[:, n % 2, :]).then_inc(e_yTc, 1)
            act.wait_ge(e_var, 1)
            nc.scalar.activation(sd[:], mv[:, :, 1], ACT.Sqrt, bias=epsln[:]).then_inc(e_sd, 1)
            for n in range(4):
                act.wait_ge(e_xT, n + 1)
                nc.scalar.copy(xn2T[:, n * BANK:(n + 1) * BANK], PS[:, n % 2, :]).then_inc(e_xTc, 1)
            for k in range(4 * HB):
                act.wait_ge(e_gu, k + 1)
                if k >= 2:
                    act.wait_ge(e_h, k - 1)
                nc.scalar.activation(sil[:, k % 2, :], PS[:, 2 + 2 * (k % 2), :], ACT.Silu).then_inc(e_sil, 1)

        @block.vector
        def _(dve):
            steps = [0]

            def step(ins):
                steps[0] += 1
                ins.then_inc(dve_s, 1)
                dve.wait_ge(dve_s, steps[0])

            nc.vector.memset(epsln[:], EPS_LN)
            nc.vector.memset(mhalf[:], -0.5)
            nc.vector.memset(phalf[:], 0.5)
            nc.vector.memset(PS[:, 6:8, :], 0.0).then_inc(y_norm, 1)

            for t in range(TT):
                if t % 4 == 0:
                    dve.wait_ge(x_in[t // 4], 16)
                last = nc.vector.bn_stats(st6[:, t, :], xres[:, t, :])
            step(last)
            for t in range(TT):
                last = nc.vector.bn_aggr(mv[:, t, :], st6[:, t, :])
            last.then_inc(var_ready, 1)
            dve.wait_ge(sd_ready, 1)
            step(nc.vector.reciprocal(rstd[:], sd[:]))
            for t in range(TT):
                last = nc.vector.tensor_scalar(xn[:, t, :], xres[:, t, :], mv[:, t, 0:1], rstd[:, t:t + 1],
                                               ALU.subtract, ALU.mult).then_inc(xn_ready, 1)
            dve.wait_ge(w_in, 80)
            dve.wait_ge(consts, 2)
            v9 = V9[:].rearrange("p (b q) (t u w) -> p b q t u w", b=B, t=NT, u=U)
            for t in range(TT):
                pq = PS[:, 2 + t % 4, :]
                dve.wait_ge(qkv_ready, t + 1)
                nc.vector.tensor_tensor(uq[:, t, :], pq[:, 0:2 * C], Wb[:, 0:2 * C], ALU.add)
                nc.vector.tensor_tensor(v9[:, t // NT, :, t % NT, :, 0:D],
                                        pq[:, 2 * C:3 * C].rearrange("p (q u d) -> p q u d", q=QUADS, u=U),
                                        Wb[:, 2 * C:3 * C].rearrange("p (q u d) -> p q u d", q=QUADS, u=U), ALU.add)
                nc.vector.tensor_tensor(sur[:, t:t + 1], pq[:, 3 * C:NW], Wb[:, 3 * C:NW],
                                        ALU.add).then_inc(qkv_used, 1)
            dve.wait_ge(wo_in, 32)
            nc.vector.tensor_tensor(xres[:], xres[:], bo[:].unsqueeze(1).to_broadcast([P, TT, C]),
                                    ALU.add).then_inc(sur_ready, 1)
            us = usq.rearrange("p (m d) -> p m d", d=D)
            dve.wait_ge(usq_ready, 2)
            step(nc.vector.tensor_reduce(mk, us[:, :, 1:D], AX.X, ALU.add))
            step(nc.vector.tensor_tensor(mk, mk, us[:, :, 0], ALU.subtract))
            nc.vector.tensor_scalar(mk, mk, 1e-8, None, ALU.max).then_inc(mk_ready, 1)
            dve.wait_ge(mk_ready, 1)
            step(nc.vector.tensor_scalar(mc, mk, 1.0, None, ALU.min))
            for dst, cf in ((p1, COSH), (p2, SINH)):
                step(nc.vector.tensor_scalar(dst, mc, cf[-1], None, ALU.mult))
                for c in cf[-2::-1]:
                    step(nc.vector.scalar_tensor_tensor(dst, dst, c, mc, ALU.add, ALU.mult))
                step(nc.vector.tensor_scalar(dst, dst, 1.0, None, ALU.add))
            dve.wait_ge(root_ready, 1)
            step(nc.vector.reciprocal(rn, n0))
            step(nc.vector.tensor_tensor(rn, rn, mk, ALU.mult))
            nc.vector.tensor_tensor(n2, rn, n0, ALU.add).then_inc(n2_ready, 1)
            dve.wait_ge(n2_ready, 1)
            step(nc.vector.reciprocal(rn, n2))
            dve.wait_ge(ex_ready, 1)
            step(nc.vector.reciprocal(ei, ex))
            step(nc.vector.tensor_tensor(sh, ex, ei, ALU.subtract))
            step(nc.vector.tensor_tensor(co, sh, rn, ALU.mult))
            step(nc.vector.tensor_tensor(ch, ex, ei, ALU.add))
            step(nc.vector.tensor_scalar(cs, ch, 0.5, None, ALU.mult))
            step(nc.vector.tensor_scalar(msk, mk, 1.0, None, ALU.is_lt))
            step(nc.vector.copy_predicated(co, msk, p2))
            step(nc.vector.copy_predicated(cs, msk, p1))
            coq = co.rearrange("p (t s h) -> p t s h", t=TT, s=2)[:, :, 0, :]
            step(nc.vector.tensor_scalar(coq, coq, -1.0, None, ALU.mult))
            um = uq.rearrange("p t c -> p (t c)").rearrange("p (m d) -> p m d", d=D)
            for n in range(4):
                m = slice(128 * n, 128 * (n + 1))
                nc.vector.tensor_tensor(um[:, m, 1:D], um[:, m, 1:D],
                                        co[:, m].unsqueeze(2).to_broadcast([P, 128, D - 1]), ALU.mult)
                nc.vector.tensor_copy(um[:, m, 0], cs[:, m]).then_inc(hat_ready, 1)
            for k in range(8):
                n, s = k // 2, k % 2
                cols = slice(n * BANK, (n + 1) * BANK)
                dve.wait_ge(h1_ready, k + 1)
                nc.vector.tensor_tensor(rem[:, k % 2, :], PS[:, k % 4, :], split[:, s, 0, cols],
                                        ALU.subtract).then_inc(r1_ready, 1)
                dve.wait_ge(h2_ready, k + 1)
                dve.wait_ge(r1_ready, k + 1)
                nc.vector.tensor_tensor(split[:, s, 2, cols], rem[:, k % 2, :], split[:, s, 1, cols],
                                        ALU.subtract).then_inc(h3_ready, 1)
            dve.wait_ge(sg_ready, 1)
            step(nc.vector.tensor_scalar(sg[:], sg[:], 1.0, None, ALU.add))
            step(nc.vector.reciprocal(sg[:], sg[:]))
            for b in range(B):
                step(nc.vector.tensor_scalar(
                    spike[:, b * QUADS:(b + 1) * QUADS, :],
                    sg[:, b * NT:(b + 1) * NT].unsqueeze(1).to_broadcast([P, QUADS, NT]),
                    thr[:], None, ALU.is_gt))

            def clamp(g, u, t):
                w = (t + 1) * P
                bank = 2 * (t % 2)
                dve.wait_ge(z_ready, g * (U * NT) + (u * NT + t + 1))
                nc.vector.tensor_scalar(Z[:, u, OFF[t]:OFF[t] + w],
                                        PS[:, bank:bank + 2, :].rearrange("p b c -> p (b c)")[:, 0:w],
                                        ONE_EPS, None, ALU.max, ALU.min,
                                        accum_out=Z[:, u, FU + t:FU + t + 1]).then_inc(z_used, 1)

            def square(g, u, lo, hi):
                return nc.vector.tensor_tensor(Z[:, u, lo:hi], Z[:, u, lo:hi], Z[:, u, lo:hi], ALU.mult)

            def group(g, nxt):
                for u in range(U):
                    dve.wait_ge(roots_ready, g * U + (u + 1))
                    nc.vector.tensor_tensor(Z[:, u, :], Z[:, u, :], X[:, u % 2, :], ALU.add).then_inc(sum_ready, 1)
                for u in range(3):
                    dve.wait_ge(log_ready, g * U + (u + 1))
                    square(g, u, 0, FB).then_inc(sq_ready, 1)
                if nxt:
                    dve.wait_ge(t_ready, g * (U * NCH) + NCH)
                    clamp(g + 1, 0, 0)
                    clamp(g + 1, 0, 1)
                dve.wait_ge(log_ready, g * U + U)
                cut = [0, FB // 4, FB // 2, 3 * FB // 4, FB]
                for i in range(4):
                    last = square(g, 3, cut[i], cut[i + 1])
                    if i == 3:
                        last.then_inc(sq_ready, 1)
                    if nxt and i < 3:
                        clamp(g + 1, 0, 2 + 2 * i)
                        clamp(g + 1, 0, 3 + 2 * i)
                if nxt:
                    for u in (1, 2):
                        dve.wait_ge(t_ready, g * (U * NCH) + (u + 1) * NCH)
                        for t in range(NT):
                            clamp(g + 1, u, t)
                dve.wait_ge(pv_done, g * (U * NCH) + U * NCH)
                nc.vector.tensor_copy(yS[:], PS[:, 6:8, :].rearrange("p b c -> p (b c)")).then_inc(o_saved, 1)
                if nxt:
                    for t in range(NT):
                        clamp(g + 1, 3, t)
                yt = PS[:, 4:6, :].rearrange("p b c -> p (b c)").rearrange("p (t u r) -> p t u r", t=NT, u=U)
                dve.wait_ge(yT_ready, g + 1)
                nc.vector.reciprocal(den[:], yt[:, :, :, D]).then_inc(den_step, 1)
                dve.wait_ge(den_step, 2 * g + 1)
                nc.vector.tensor_tensor(
                    den[:], den[:],
                    spike[:].rearrange("p g t -> p (g t)")[:, bass.ds(g * NT, NT)].unsqueeze(2).to_broadcast([P, NT, U]),
                    ALU.mult).then_inc(den_step, 1)
                dve.wait_ge(den_step, 2 * g + 2)
                yg = Y[:].rearrange("p (b t) (q w) -> p b q t w", b=B, q=QUADS)
                nc.vector.tensor_tensor(
                    yg[:, bass.ds(g // QUADS, 1), bass.ds(g % QUADS, 1), :, :].rearrange(
                        "p b q t (u d) -> p (b q t) u d", u=U), yt[:, :, :, 0:D],
                    den[:].unsqueeze(3).to_broadcast([P, NT, U, D]), ALU.mult).then_inc(y_norm, 1)

            for u in range(U):
                for t in range(NT):
                    clamp(0, u, t)
            with dve.Fori(0, G - 1) as g:
                group(g, True)
            group(G - 1, False)

            for n in range(4):
                dve.wait_ge(e_at, n + 1)
                nc.vector.tensor_tensor(x1[:, 4 * n:4 * n + 4, :].rearrange("p t c -> p (t c)"), PS[:, 2 + n, :],
                                        xres[:, 4 * n:4 * n + 4, :].rearrange("p t c -> p (t c)"),
                                        ALU.add).then_inc(e_x1, 1)
            dve.wait_ge(e_x1, 4)
            for t in range(TT):
                last = nc.vector.bn_stats(st6[:, t, :], x1[:, t, :])
            step(last)
            for t in range(TT):
                last = nc.vector.bn_aggr(mv[:, t, :], st6[:, t, :])
            last.then_inc(e_var, 1)
            dve.wait_ge(e_sd, 1)
            step(nc.vector.reciprocal(rstd[:], sd[:]))
            for t in range(TT):
                nc.vector.tensor_scalar(xn2[:, t, :], x1[:, t, :], mv[:, t, 0:1], rstd[:, t:t + 1],
                                        ALU.subtract, ALU.mult).then_inc(e_xn, 1)

            def ffn_out(n):
                dve.wait_ge(e_dn, n + 1)
                nc.vector.tensor_tensor(res[:, n].rearrange("p t c -> p (t c)"), PS[:, 6 + n % 2, :],
                                        x1[:, 4 * n:4 * n + 4, :].rearrange("p t c -> p (t c)"),
                                        ALU.add).then_inc(e_res, 1)

            for n in range(4):
                for a in range(HB):
                    k = n * HB + a
                    dve.wait_ge(e_sil, k + 1)
                    if n >= 2 and a == 0:
                        dve.wait_ge(e_dn, n - 1)
                    nc.vector.tensor_tensor(hT[:, n % 2, a, :], sil[:, k % 2, :], PS[:, 3 + 2 * (k % 2), :],
                                            ALU.mult).then_inc(e_h, 1)
                if n >= 1:
                    ffn_out(n - 1)
            ffn_out(3)

        @block.tensor
        def _(pe):
            mm = nc.tensor.matmul

            def transposes(bank, srcs):
                for i, src in enumerate(srcs):
                    last = nc.tensor.transpose(PS[:, bank, i * P:(i + 1) * P], src, ident[:])
                return last

            pe.wait_ge(consts, 5)
            for n in range(4):
                pe.wait_ge(xn_ready, 4 * n + 4)
                if n >= 2:
                    pe.wait_ge(tr_copied, n - 1)
                transposes(n % 2, [xn[:, 4 * n + i, :] for i in range(4)]).then_inc(tr_ready, 1)
            pe.wait_ge(w_in, 80)
            for t in range(TT):
                pe.wait_ge(tr_copied, t // 4 + 1)
                if t >= 4:
                    pe.wait_ge(qkv_used, t - 3)
                mm(PS[:, 2 + t % 4, 0:NW], xnT[:, t * P:(t + 1) * P], W[:], start=True, stop=True
                   ).then_inc(qkv_ready, 1)
            pe.wait_ge(wf_ready, 1)
            for n in range(3):
                pe.wait_ge(tr_copied, n + 3)
                transposes(n % 2, [wf[:, (HB * n + a) * P:(HB * n + a + 1) * P] for a in range(HB)]
                           ).then_inc(tr_ready, 1)
            pe.wait_ge(tr_copied, 7)
            for k in range(8):
                n, s = k // 2, k % 2
                pe.wait_ge(hat_ready, n + 1)
                if k >= 4:
                    pe.wait_ge(r1_ready, k - 3)
                transposes(k % 4, [uq[:, 4 * n + i, s * C:(s + 1) * C] for i in range(4)]).then_inc(hatT_ready, 1)

            def scores(g, u, t, first=False):
                e, pr, bank = ROWS * (u % 2), u // 2, 2 * (t % 2)
                if t == 0:
                    pe.wait_ge(stacks[u], g * NSTK + NSTK)
                if not (first and u * NT + t < 2):
                    pe.wait_ge(z_used, g * (U * NT) + (u * NT + t - 1))
                lhs = Qs[e:e + ROWS, pr, t * P:(t + 1) * P]
                for c in range(t // 4 + 1):
                    w = min((t + 1) * P - c * BANK, BANK)
                    mm(PS[:, bank + c, 0:w], lhs, Ks[e:e + ROWS, pr, c * BANK:c * BANK + w], start=True, stop=True)
                d = (t % 4) * P
                mm(PS[:, bank + t // 4, d:d + P], identb[:], maskb[:], start=False, stop=True,
                   skip_group_check=True).then_inc(z_ready, 1)

            def transposed(g, n):
                u, (c, jt) = n // NCH, CH[n % NCH]
                bank = 4 + n % NTB
                if n % NCH == 0:
                    pe.wait_ge(sq_ready, g * U + (u + 1))
                if n >= NTB:
                    pe.wait_ge(p_ready, g * (U * NCH) + (n + 1 - NTB))
                t0 = max(jt, 4 * c)
                for t in range(t0, 4 * c + 4):
                    o = (t - 4 * c) * P
                    mm(PS[:, bank, o:o + P], Z[:, u, OFF[t] + jt * P:OFF[t] + (jt + 1) * P], ident[:],
                       is_transpose=True, start=(t == t0), stop=True, skip_group_check=True)
                if n % NCH == 0:
                    pe.wait_ge(diag_ready, g * U + (u + 1))
                o = (t0 - 4 * c) * P
                mm(PS[:, bank, o:BANK], onesb[:], Dg[:, u % 2, t0:4 * c + 4, :], start=False, stop=True,
                   skip_group_check=True).then_inc(t_ready, 1)

            def values(g, n):
                u, (c, jt) = n // NCH, CH[n % NCH]
                o = max(jt - 4 * c, 0) * P
                pe.wait_ge(p_ready, g * (U * NCH) + (n + 1))
                mm(PS[32 * u:32 * u + VW, 6 + c, o:BANK], Vg[:, jt, u, :], PT[:, n % NPT, o:BANK],
                   start=(jt == 0), stop=(jt == 4 * c + 3), skip_group_check=True).then_inc(pv_done, 1)

            def group(g, nxt):
                hooks = {}
                for v in range(3):
                    for t in range(NT):
                        hooks[NCH * (v + 1) + (0, 1, 3, 4, 6, 7, 9, 10)[t]] = (v, t)
                pe.wait_ge(y_norm, g + 1)
                pe.wait_ge(v_ready, g + 1)
                for n in range(NTB):
                    transposed(g, n)
                for n in range(U * NCH):
                    if n + NTB < U * NCH:
                        transposed(g, n + NTB)
                    values(g, n)
                    if nxt and n in hooks:
                        scores(g + 1, *hooks[n])
                if nxt:
                    scores(g + 1, 3, 0)
                    scores(g + 1, 3, 1)
                pe.wait_ge(o_saved, g + 1)
                for t in range(NT):
                    last = nc.tensor.transpose(PS[:, 4 + t // 4, (t % 4) * P:(t % 4 + 1) * P],
                                               yS[:, t * P:(t + 1) * P], ident[:])
                last.then_inc(yT_ready, 1)
                if nxt:
                    for t in range(2, NT):
                        scores(g + 1, 3, t)

            for u in range(U):
                for t in range(NT):
                    scores(0, u, t, first=True)
            with pe.Fori(0, G - 1) as g:
                group(g, True)
            group(G - 1, False)

            pe.wait_ge(y_norm, G + 1)
            for n in range(4):
                if n >= 2:
                    pe.wait_ge(e_yTc, n - 1)
                transposes(n % 2, [Y[:, 4 * n + i, :] for i in range(4)]
                           ).then_inc(e_yT, 1)
            for n in range(4):
                pe.wait_ge(e_yTc, n + 1)
                for i in range(4):
                    t = 4 * n + i
                    last = mm(PS[:, 2 + n, i * P:(i + 1) * P], yT[:, t * P:(t + 1) * P], Wo[:], start=True, stop=True)
                last.then_inc(e_at, 1)
            for n in range(4):
                pe.wait_ge(e_xn, 4 * n + 4)
                if n >= 2:
                    pe.wait_ge(e_xTc, n - 1)
                transposes(n % 2, [xn2[:, 4 * n + i, :] for i in range(4)]).then_inc(e_xT, 1)

            def down(n):
                pe.wait_ge(e_h, HB * (n + 1))
                if n >= 2:
                    pe.wait_ge(e_res, n - 1)
                for i in range(4):
                    for a in range(HB):
                        last = mm(PS[:, 6 + n % 2, i * P:(i + 1) * P], hT[:, n % 2, a, i * P:(i + 1) * P],
                                  wT[:, 2 * HB + a, :], start=(a == 0), stop=(a == HB - 1))
                last.then_inc(e_dn, 1)

            for n in range(4):
                pe.wait_ge(e_xTc, n + 1)
                for a in range(HB):
                    k = n * HB + a
                    if k >= 2:
                        pe.wait_ge(e_h, k - 1)
                    cols = slice(n * BANK, (n + 1) * BANK)
                    mm(PS[:, 2 + 2 * (k % 2), :], wT[:, a, :], xn2T[:, cols], start=True, stop=True)
                    mm(PS[:, 3 + 2 * (k % 2), :], wT[:, HB + a, :], xn2T[:, cols], start=True, stop=True
                       ).then_inc(e_gu, 1)
                if n >= 1:
                    down(n - 1)
            down(3)


_INS = ['L0_attn_x', 'L0_attn_W_qkv', 'L0_attn_b_qkv', 'L0_attn_W_out', 'L0_attn_b_out', 'L0_attn_w_sur',
        'L0_attn_b_sur', 'L0_attn_threshold', 'L0_ffn_w_gate', 'L0_ffn_w_up', 'L0_ffn_w_down']


def kernel(**inputs):
    import numpy as _np
    import concourse.bacc as _bacc
    from concourse import mybir as _mybir
    from concourse.bass_utils import run_bass_kernel_spmd as _run

    nc = _bacc.Bacc("TRN2", target_bir_lowering=False, num_devices=1)
    arrays, args = {}, []
    for name in _INS:
        a = _np.ascontiguousarray(inputs[name])
        if a.ndim == 0:
            a = a.reshape(1)
        arrays[f"in_{name}"] = a
        args.append(nc.dram_tensor(f"in_{name}", a.shape, _mybir.dt.from_np(a.dtype), kind="ExternalInput").ap())
    args.append(nc.dram_tensor("out_0", (B, T, C), _mybir.dt.float32, kind="ExternalOutput").ap())
    layer(nc, *args)
    r = _run(nc, [arrays], core_ids=[0])
    return r.results[0]["out_0"]
```

```python
import numpy as np
import concourse.bass as bass
from concourse import mybir
from contextlib import ExitStack

fp32 = mybir.dt.float32
bf16 = mybir.dt.bfloat16
i32 = mybir.dt.int32
ALU = mybir.AluOpType
ACT = mybir.ActivationFunctionType
AX = mybir.AxisListType

P = 128
B, T, C, H, HID = 2, 1024, 128, 16, 384
D = C // H
NT = T // P
TT = B * NT
U = 4
G = B * H // U
QUADS = H // U
BANK = 512
OFF = [t * (t + 1) // 2 * P for t in range(NT + 1)]
FU = OFF[NT]
FB = FU + NT
ZW = FB + NT // 2
VW = D + 1
PARTS = 3
ROWS = 64
NZB, NTB = 2, 3
Z0, T0, O0, S0 = 0, NZB, NZB + NTB, NZB + NTB + 2
PIECES = [(t, c) for t in range(NT) for c in range(t // 4 + 1)]
NP = len(PIECES)
BINS = [[(0, 0)], [(0, 1), (0, 3)], [(0, 2), (1, 6)], [(1, 0)], [(1, 1)], [(1, 2)], [(1, 3)], [(1, 4)],
        [(1, 5), (1, 7)]]
NB = len(BINS)


def width(c, jt):
    return (4 * c + 4 - max(jt, 4 * c)) * P


PLACE = {blk: (k, sum(width(*b) for b in bin_[:i])) for k, bin_ in enumerate(BINS) for i, blk in enumerate(bin_)}
VALUES = [(0, j) for j in range(4)] + [(1, j) for j in range(8)]
NSTK = 11 * 16


def unit(g, u):
    return g * U + u


def prev(g, h):
    return [(g, 0), (g, 1)] if h else [(g - 1, 2), (g - 1, 3)]


def prev2(g, h):
    return [(g - 1, 2 * h), (g - 1, 2 * h + 1)]


def after(g, h):
    return [(g + 1, 0), (g + 1, 1)] if h else [(g, 2), (g, 3)]


EPS_LN = 1e-5
ONE_EPS = float(np.float32(1.0 + 1e-7))
MASKED = 1e35
SIGMA = 2.0 ** 0.5
NW = 3 * C + 1
QKV_BANKS = (2, 3, 4, 7)
HB = HID // P
COSH = [1 / 2, 1 / 24, 1 / 720, 1 / 40320, 1 / 3628800]
SINH = [1 / 6, 1 / 120, 1 / 5040, 1 / 362880, 1 / 39916800]


def layer(nc, x, w_qkv, b_qkv, w_out, b_out, w_sur, b_sur, threshold, w_gate, w_up, w_down, out):
    with ExitStack() as ctx:
        def sb(name, shape, dt=fp32):
            return ctx.enter_context(nc.sbuf_tensor(name, shape, dt))

        def sem(name):
            return ctx.enter_context(nc.semaphore(name))

        parts = nc.dram_tensor("qk_parts", [2, B * H, PARTS * D, T], bf16, kind="Internal").ap()

        Z = sb("Z", [P, U, ZW])
        X = sb("X", [P, 2, FB])
        xres = sb("xres", [P, TT, C])
        Y = sb("Y", [P, TT, C])
        V9 = sb("V9", [P, G, NT * U * VW])
        Vg = sb("Vg", [P, NT, U, VW])
        PT = sb("PT", [P, 2, NB, BANK])
        Qs = sb("Qs", [P, 2, T], bf16)
        Ks = sb("Ks", [P, 2, T], bf16)
        Dg = sb("Dg", [P, 2, NT, P], bf16)
        yS = sb("yS", [P, 4, BANK])
        sel = sb("sel", [P, VW])
        W = sb("W", [P, NW])
        Wb = sb("Wb", [P, NW])
        Wo = sb("Wo", [P, C])
        bo = sb("bo", [P, C])
        thr = sb("thr", [P, 1])
        wT = sb("wT", [P, 3 * HB, P])
        ident = sb("ident", [P, P])
        identb = sb("identb", [P, P], bf16)
        nident = sb("nident", [P, P])
        onesb = sb("onesb", [P, P], bf16)
        maskb = sb("maskb", [P, P], bf16)
        epsln = sb("epsln", [P, 1])
        mhalf = sb("mhalf", [P, 1])
        phalf = sb("phalf", [P, 1])
        st6 = sb("st6", [P, TT, 6])
        mv = sb("mv", [P, TT, 2])
        sd = sb("sd", [P, TT])
        rstd = sb("rstd", [P, TT])
        sur = sb("sur", [P, TT])
        sg = sb("sg", [P, TT])
        spike = sb("spike", [P, G, NT])
        den = sb("den", [P, U, NT])
        PS = ctx.enter_context(nc.psum_tensor("PS", [P, 8, BANK], fp32))

        uq = X[:, 0, 0:TT * 2 * C].rearrange("p (t c) -> p t c", t=TT)
        usq = X[:, 1, 0:TT * 2 * C]
        wf = Y[:].rearrange("p t c -> p (t c)")[:, 0:3 * HB * P]
        xn = X[:, 1, 0:TT * C].rearrange("p (t c) -> p t c", t=TT)
        xnT = Z[:, 0, 0:TT * P]
        split = Z[:, 2:4, 0:PARTS * B * T // 2].bitcast(bf16).rearrange("p s (n t) -> p s n t", n=PARTS)
        small = [Z[:, 0, TT * P + 512 * i:TT * P + 512 * (i + 1)] for i in range(5)] + \
                [Z[:, 1, 512 * i:512 * (i + 1)] for i in range(9)]
        mk, mc, n0, rn, n2, ex, ei, ch, sh, co, p1, p2, cs, tmp = small
        msk = tmp.bitcast(i32)
        wint = PT[:, 1, :, :].rearrange("p k c -> p (k c)").bitcast(i32)[:, 0:3 * HB * P].rearrange(
            "p (a d) -> p a d", d=P)
        rem = PT[:, 0]
        x1 = Z[:, 0, 0:TT * C].rearrange("p (t c) -> p t c", t=TT)
        yT = Z[:, 1, 0:TT * P]
        xn2 = Z[:, 2, 0:TT * C].rearrange("p (t c) -> p t c", t=TT)
        xn2T = Z[:, 3, 0:TT * P]
        sil = X[:, 0, 0:2 * BANK].rearrange("p (n t) -> p n t", n=2)
        hT = X[:, 1, 0:2 * HB * BANK].rearrange("p (n a t) -> p n a t", n=2, a=HB)
        res = X[:, 0, 2 * BANK:6 * BANK].rearrange("p (n t c) -> p n t c", n=4, t=4)

        x_in = [sem(f"x_in{n}") for n in range(4)]
        w_in, wo_in, wi_in = sem("w_in"), sem("wo_in"), sem("wi_in")
        consts, wf_ready = sem("consts"), sem("wf_ready")
        dve_s, pool_s = sem("dve_s"), sem("pool_s")
        var_ready, sd_ready, xn_ready, tr_ready, tr_copied = (sem(n) for n in (
            "var_ready", "sd_ready", "xn_ready", "tr_ready", "tr_copied"))
        qkv_ready, qkv_used, usq_ready, mk_ready, root_ready, n2_ready, ex_ready, hat_ready = (sem(n) for n in (
            "qkv_ready", "qkv_used", "usq_ready", "mk_ready", "root_ready", "n2_ready", "ex_ready", "hat_ready"))
        sur_ready, sg_ready = sem("sur_ready"), sem("sg_ready")
        hatT_ready, h1_ready, r1_ready, h2_ready, h3_ready = (sem(n) for n in (
            "hatT_ready", "h1_ready", "r1_ready", "h2_ready", "h3_ready"))
        stored = sem("stored")
        stacks = [sem(f"stacks{u}") for u in range(U)]
        unit_in, half_summed = sem("unit_in"), sem("half_summed")
        z_ready, z_used, roots_ready, sum_ready, log_ready, sq_ready, diag_ready, v_ready = (sem(n) for n in (
            "z_ready", "z_used", "roots_ready", "sum_ready", "log_ready", "sq_ready", "diag_ready", "v_ready"))
        t_ready, p_ready, pv_done, o_saved, den_step, y_norm = (sem(n) for n in (
            "t_ready", "p_ready", "pv_done", "o_saved", "den_step", "y_norm"))
        e_yT, e_yTc, e_at, e_x1, e_var, e_sd, e_xn, e_xT, e_xTc, e_gu, e_sil, e_h, e_dn, e_res, e_out = (
            sem("e_" + n) for n in ("yT", "yTc", "at", "x1", "var", "sd", "xn", "xT", "xTc", "gu", "sil", "h",
                                    "dn", "res", "out"))

        block = ctx.enter_context(nc.Block())

        @block.sync
        def _(sp):
            xt = x.rearrange("b (t p) c -> p (b t) c", p=P)
            for n in range(4):
                sp.dma_start(xres[:, 4 * n:4 * n + 4, :], xt[:, 4 * n:4 * n + 4, :]).then_inc(x_in[n], 16)
            sp.dma_start(wint[:, 0:HB, :], w_gate.rearrange("(a p) d -> p a d", p=P)).then_inc(wi_in, 16)
            sp.dma_start(wint[:, HB:2 * HB, :], w_up.rearrange("(a p) d -> p a d", p=P)).then_inc(wi_in, 16)
            sp.dma_start(wint[:, 2 * HB:3 * HB, :], w_down.rearrange("d (a h) -> d a h", a=HB)).then_inc(wi_in, 16)

            for b in range(B):
                sp.wait_ge(h3_ready, 4 * (b + 1))
                for s in range(2):
                    for n in range(PARTS):
                        sp.dma_start(
                            parts[s, b * H:(b + 1) * H, n * D:(n + 1) * D, :],
                            split[:, s, n, b * T:(b + 1) * T]).then_inc(stored, 16)

            def load_stacks(n, u):
                r0, pr = ROWS * (u % 2), u // 2
                for first, reps, part in ((0, 3, 0), (24, 3, 1), (48, 2, 2)):
                    src = parts[0, bass.ds(n, 1), part * D:(part + 1) * D, :].rearrange("o d t -> (o d) t")
                    for rep in range(reps):
                        a = r0 + first + rep * D
                        sp.dma_start(Qs[a:a + D, pr, :], src).then_inc(stacks[u], 16)
                for first, rows in ((0, 24), (24, 24), (48, 16)):
                    src = parts[1, bass.ds(n, 1), 0:rows, :].rearrange("o d t -> (o d) t")
                    sp.dma_start(Ks[r0 + first:r0 + first + rows, pr, :], src).then_inc(stacks[u], 16)

            sp.wait_ge(stored, 16 * 2 * PARTS * B)
            for u in range(U):
                load_stacks(u, u)
            with sp.Fori(0, G - 1) as g:
                for u in range(U):
                    sp.wait_ge(z_ready, g * (U * NP) + (u + 1) * NP)
                    load_stacks(g * U + (U + u), u)

            ot = out.rearrange("b (t p) c -> p (b t) c", p=P)
            for n in range(4):
                sp.wait_ge(e_res, n + 1)
                sp.dma_start(ot[:, 4 * n:4 * n + 4, :], res[:, n]).then_inc(e_out, 16)
            sp.wait_ge(e_out, 64)

        @block.gpsimd
        def _(pool):
            nc.gpsimd.memset(ident[:], 0.0).then_inc(pool_s, 1)
            nc.gpsimd.memset(maskb[:], 0.0).then_inc(pool_s, 1)
            nc.gpsimd.memset(V9[:], 1.0).then_inc(consts, 1)
            nc.gpsimd.memset(onesb[:], 1.0).then_inc(consts, 1)
            pool.wait_ge(pool_s, 2)
            nc.gpsimd.affine_select(out=ident[:], in_=ident[:], compare_op=ALU.not_equal, fill=1.0, base=0,
                                    pattern=[[-1, P]], channel_multiplier=1).then_inc(pool_s, 1)
            nc.gpsimd.affine_select(out=maskb[:], in_=maskb[:], compare_op=ALU.is_ge, fill=MASKED, base=0,
                                    pattern=[[-1, P]], channel_multiplier=1).then_inc(consts, 1)
            pool.wait_ge(pool_s, 3)
            nc.gpsimd.tensor_copy(identb[:], ident[:]).then_inc(consts, 1)
            nc.gpsimd.tensor_scalar(nident[:], ident[:], -1.0, 0.0, ALU.mult, ALU.add).then_inc(consts, 1)
            pool.wait_ge(wi_in, 48)
            nc.gpsimd.tensor_scalar(wf, wint.rearrange("p a d -> p (a d)"),
                                    float(np.float32(1.0 / 127.0)), 0.0, ALU.mult, ALU.add).then_inc(wf_ready, 1)

            pool.wait_ge(qkv_used, TT)

            def pool_group(g, first=False):
                for u in range(U):
                    if u == 2:
                        if not first:
                            pool.wait_ge(pv_done, unit(g, 0) * 3)
                        nc.gpsimd.tensor_copy(
                            Vg[:].rearrange("p t u w -> p (t u w)"),
                            V9[:].rearrange("p g w -> p (g w)")[:, bass.ds(g * (NT * U * VW), NT * U * VW)]
                        ).then_inc(v_ready, 1)
                    if u >= 2 or not first:
                        pool.wait_ge(t_ready, (unit(g, u) - 1) * NB)
                    pool.wait_ge(sq_ready, unit(g, u) + 1)
                    nc.gpsimd.tensor_tensor(
                        Dg[:, u % 2], nident[:].unsqueeze(1).to_broadcast([P, NT, P]),
                        Z[:, u, FU:FB].unsqueeze(2).to_broadcast([P, NT, P]), ALU.mult).then_inc(diag_ready, 1)

            pool_group(0, first=True)
            with pool.Fori(1, G) as g:
                pool_group(g)

        @block.scalar
        def _(act):
            act.dma_start(W[:, 0:3 * C], w_qkv).then_inc(w_in, 16)
            act.dma_start(W[:, 3 * C:NW], w_sur.unsqueeze(1)).then_inc(w_in, 16)
            act.dma_start(Wb[:, 0:3 * C], b_qkv.partition_broadcast(P)).then_inc(w_in, 16)
            act.dma_start(Wb[:, 3 * C:NW], b_sur.partition_broadcast(P)).then_inc(w_in, 16)
            act.dma_start(thr[:], threshold.partition_broadcast(P)).then_inc(w_in, 16)
            act.dma_start(Wo[:], w_out).then_inc(wo_in, 16)
            act.dma_start(bo[:], b_out.partition_broadcast(P)).then_inc(wo_in, 16)

            act.wait_ge(var_ready, 1)
            nc.scalar.activation(sd[:], mv[:, :, 1], ACT.Sqrt, bias=epsln[:]).then_inc(sd_ready, 1)
            for n in range(4):
                act.wait_ge(tr_ready, n + 1)
                nc.scalar.copy(xnT[:, n * BANK:(n + 1) * BANK], PS[:, n % 2, :]).then_inc(tr_copied, 1)
            for n in range(3):
                act.wait_ge(tr_ready, n + 5)
                nc.scalar.copy(wT[:, HB * n:HB * (n + 1), :].rearrange("p a d -> p (a d)"),
                               PS[:, n % 2, 0:HID]).then_inc(tr_copied, 1)
            for b in range(B):
                act.wait_ge(qkv_used, NT * (b + 1))
                w = NT * 2 * C
                nc.scalar.activation(usq[:, b * w:(b + 1) * w],
                                     uq[:, b * NT:(b + 1) * NT, :].rearrange("p t c -> p (t c)"),
                                     ACT.Square).then_inc(usq_ready, 1)
            act.wait_ge(mk_ready, 1)
            nc.scalar.activation(n0, mk, ACT.Sqrt).then_inc(root_ready, 1)
            act.wait_ge(n2_ready, 1)
            nc.scalar.activation(ex, n2, ACT.Exp, scale=0.5).then_inc(ex_ready, 1)
            act.wait_ge(sur_ready, 1)
            nc.scalar.activation(sg[:], sur[:], ACT.Exp, scale=-1.0).then_inc(sg_ready, 1)
            for k in range(8):
                n, s = k // 2, k % 2
                act.wait_ge(hatT_ready, k + 1)
                nc.scalar.copy(split[:, s, 0, n * BANK:(n + 1) * BANK], PS[:, k % 4, :]).then_inc(h1_ready, 1)
                act.wait_ge(r1_ready, k + 1)
                nc.scalar.copy(split[:, s, 1, n * BANK:(n + 1) * BANK], rem[:, k % 2, :]).then_inc(h2_ready, 1)

            def log(g, u):
                act.wait_ge(sum_ready, unit(g, u) + 1)
                nc.scalar.activation(Z[:, u, 0:FB], Z[:, u, 0:FB], ACT.Ln).then_inc(log_ready, 1)

            def roots(g, u):
                act.wait_ge(unit_in, unit(g, u) + 1)
                nc.scalar.activation(X[:, u % 2, :], Z[:, u, 0:FB], ACT.Sqrt, scale=0.5, bias=mhalf[:])
                nc.scalar.activation(Z[:, u, 0:FB], Z[:, u, 0:FB], ACT.Sqrt, scale=0.5, bias=phalf[:]
                                     ).then_inc(roots_ready, 1)

            def exps(g, u, first=False):
                for k in range(NB):
                    act.wait_ge(t_ready, unit(g, u) * NB + (k + 1))
                    if k in (0, 2, 3, 7) and not first:
                        act.wait_ge(pv_done, (unit(g, u) - 2) * 3 + {0: 1, 2: 3, 3: 2, 7: 3}[k])
                    nc.scalar.activation(PT[:, u % 2, k, :], PS[:, T0 + k % NTB, :], ACT.Exp,
                                         scale=-SIGMA).then_inc(p_ready, 1)

            def act_step(g, h, begin=False, first=False, end=False):
                if not end:
                    roots(g, 2 * h)
                    roots(g, 2 * h + 1)
                nc.scalar.preload_act_table_set("natural_log_exp_and_others")
                if not begin:
                    exps(*prev(g, h)[0], first=first)
                if not end:
                    log(g, 2 * h)
                    log(g, 2 * h + 1)
                if not begin:
                    exps(*prev(g, h)[1], first=first)

            act_step(0, 0, begin=True)
            act_step(0, 1, first=True)
            with act.Fori(1, G) as g:
                act_step(g, 0)
                act_step(g, 1)
            act_step(G, 0, end=True)

            for n in range(4):
                act.wait_ge(e_yT, n + 1)
                nc.scalar.copy(yT[:, n * BANK:(n + 1) * BANK], PS[:, n % 2, :]).then_inc(e_yTc, 1)
            act.wait_ge(e_var, 1)
            nc.scalar.activation(sd[:], mv[:, :, 1], ACT.Sqrt, bias=epsln[:]).then_inc(e_sd, 1)
            for n in range(4):
                act.wait_ge(e_xT, n + 1)
                nc.scalar.copy(xn2T[:, n * BANK:(n + 1) * BANK], PS[:, n % 2, :]).then_inc(e_xTc, 1)
            for k in range(4 * HB):
                act.wait_ge(e_gu, k + 1)
                if k >= 2:
                    act.wait_ge(e_h, k - 1)
                nc.scalar.activation(sil[:, k % 2, :], PS[:, 2 + 2 * (k % 2), :], ACT.Silu).then_inc(e_sil, 1)

        @block.vector
        def _(dve):
            steps = [0]

            def step(ins):
                steps[0] += 1
                ins.then_inc(dve_s, 1)
                dve.wait_ge(dve_s, steps[0])

            nc.vector.memset(epsln[:], EPS_LN)
            nc.vector.memset(mhalf[:], -0.5)
            nc.vector.memset(phalf[:], 0.5)
            nc.vector.memset(PS[:, O0:O0 + 2, :], 0.0).then_inc(y_norm, 1)

            for t in range(TT):
                if t % 4 == 0:
                    dve.wait_ge(x_in[t // 4], 16)
                last = nc.vector.bn_stats(st6[:, t, :], xres[:, t, :])
            step(last)
            for t in range(TT):
                last = nc.vector.bn_aggr(mv[:, t, :], st6[:, t, :])
            last.then_inc(var_ready, 1)
            dve.wait_ge(sd_ready, 1)
            step(nc.vector.reciprocal(rstd[:], sd[:]))
            for t in range(TT):
                last = nc.vector.tensor_scalar(xn[:, t, :], xres[:, t, :], mv[:, t, 0:1], rstd[:, t:t + 1],
                                               ALU.subtract, ALU.mult).then_inc(xn_ready, 1)
            dve.wait_ge(w_in, 80)
            dve.wait_ge(consts, 5)
            for q in range(4):
                nc.vector.tensor_copy(sel[32 * q:32 * q + 32, :], ident[32 * q:32 * q + 32, 32 * q:32 * q + VW])
            v9 = V9[:].rearrange("p (b q) (t u w) -> p b q t u w", b=B, t=NT, u=U)
            for t in range(TT):
                pq = PS[:, QKV_BANKS[t % 4], :]
                dve.wait_ge(qkv_ready, t + 1)
                nc.vector.tensor_tensor(uq[:, t, :], pq[:, 0:2 * C], Wb[:, 0:2 * C], ALU.add)
                nc.vector.tensor_tensor(v9[:, t // NT, :, t % NT, :, 0:D],
                                        pq[:, 2 * C:3 * C].rearrange("p (q u d) -> p q u d", q=QUADS, u=U),
                                        Wb[:, 2 * C:3 * C].rearrange("p (q u d) -> p q u d", q=QUADS, u=U), ALU.add)
                nc.vector.tensor_tensor(sur[:, t:t + 1], pq[:, 3 * C:NW], Wb[:, 3 * C:NW],
                                        ALU.add).then_inc(qkv_used, 1)
            dve.wait_ge(wo_in, 32)
            nc.vector.tensor_tensor(xres[:], xres[:], bo[:].unsqueeze(1).to_broadcast([P, TT, C]),
                                    ALU.add).then_inc(sur_ready, 1)
            us = usq.rearrange("p (m d) -> p m d", d=D)
            dve.wait_ge(usq_ready, 2)
            step(nc.vector.tensor_reduce(mk, us[:, :, 1:D], AX.X, ALU.add))
            step(nc.vector.tensor_tensor(mk, mk, us[:, :, 0], ALU.subtract))
            nc.vector.tensor_scalar(mk, mk, 1e-8, None, ALU.max).then_inc(mk_ready, 1)
            dve.wait_ge(mk_ready, 1)
            step(nc.vector.tensor_scalar(mc, mk, 1.0, None, ALU.min))
            for dst, cf in ((p1, COSH), (p2, SINH)):
                step(nc.vector.tensor_scalar(dst, mc, cf[-1], None, ALU.mult))
                for c in cf[-2::-1]:
                    step(nc.vector.scalar_tensor_tensor(dst, dst, c, mc, ALU.add, ALU.mult))
                step(nc.vector.tensor_scalar(dst, dst, 1.0, None, ALU.add))
            dve.wait_ge(root_ready, 1)
            step(nc.vector.reciprocal(rn, n0))
            step(nc.vector.tensor_tensor(rn, rn, mk, ALU.mult))
            nc.vector.tensor_tensor(n2, rn, n0, ALU.add).then_inc(n2_ready, 1)
            dve.wait_ge(n2_ready, 1)
            step(nc.vector.reciprocal(rn, n2))
            dve.wait_ge(ex_ready, 1)
            step(nc.vector.reciprocal(ei, ex))
            step(nc.vector.tensor_tensor(sh, ex, ei, ALU.subtract))
            step(nc.vector.tensor_tensor(co, sh, rn, ALU.mult))
            step(nc.vector.tensor_tensor(ch, ex, ei, ALU.add))
            step(nc.vector.tensor_scalar(cs, ch, 0.5, None, ALU.mult))
            step(nc.vector.tensor_scalar(msk, mk, 1.0, None, ALU.is_lt))
            step(nc.vector.copy_predicated(co, msk, p2))
            step(nc.vector.copy_predicated(cs, msk, p1))
            coq = co.rearrange("p (t s h) -> p t s h", t=TT, s=2)[:, :, 0, :]
            step(nc.vector.tensor_scalar(coq, coq, -1.0, None, ALU.mult))
            um = uq.rearrange("p t c -> p (t c)").rearrange("p (m d) -> p m d", d=D)
            for n in range(4):
                m = slice(128 * n, 128 * (n + 1))
                nc.vector.tensor_tensor(um[:, m, 1:D], um[:, m, 1:D],
                                        co[:, m].unsqueeze(2).to_broadcast([P, 128, D - 1]), ALU.mult)
                nc.vector.tensor_copy(um[:, m, 0], cs[:, m]).then_inc(hat_ready, 1)
            for k in range(8):
                n, s = k // 2, k % 2
                cols = slice(n * BANK, (n + 1) * BANK)
                dve.wait_ge(h1_ready, k + 1)
                nc.vector.tensor_tensor(rem[:, k % 2, :], PS[:, k % 4, :], split[:, s, 0, cols],
                                        ALU.subtract).then_inc(r1_ready, 1)
                dve.wait_ge(h2_ready, k + 1)
                dve.wait_ge(r1_ready, k + 1)
                nc.vector.tensor_tensor(split[:, s, 2, cols], rem[:, k % 2, :], split[:, s, 1, cols],
                                        ALU.subtract).then_inc(h3_ready, 1)
            dve.wait_ge(sg_ready, 1)
            step(nc.vector.tensor_scalar(sg[:], sg[:], 1.0, None, ALU.add))
            step(nc.vector.reciprocal(sg[:], sg[:]))
            for b in range(B):
                step(nc.vector.tensor_scalar(
                    spike[:, b * QUADS:(b + 1) * QUADS, :],
                    sg[:, b * NT:(b + 1) * NT].unsqueeze(1).to_broadcast([P, QUADS, NT]),
                    thr[:], None, ALU.is_gt))

            def clamp(g, u, i):
                t, c = PIECES[i]
                w = min((t + 1) * P - c * BANK, BANK)
                own, col = OFF[t] + c * BANK, FU + t + c * NT // 2
                if t < 4:
                    col = FU + t
                dve.wait_ge(z_ready, g * (U * NP) + (u * NP + i + 1))
                nc.vector.tensor_scalar(Z[:, u, own:own + w], PS[:, Z0 + i % NZB, 0:w], ONE_EPS, None, ALU.max,
                                        ALU.min, accum_out=Z[:, u, col:col + 1]).then_inc(z_used, 1)
                if i == NP - 1:
                    dve.wait_ge(z_used, g * (U * NP) + (u + 1) * NP)
                    nc.vector.tensor_tensor(Z[:, u, FU + 4:FB], Z[:, u, FU + 4:FB], Z[:, u, FB:ZW],
                                            ALU.min).then_inc(unit_in, 1)

            def add_roots(g, u):
                dve.wait_ge(roots_ready, g * U + (u + 1))
                nc.vector.tensor_tensor(Z[:, u, 0:FB], Z[:, u, 0:FB], X[:, u % 2, :], ALU.add).then_inc(sum_ready, 1)

            def square(g, u):
                dve.wait_ge(log_ready, g * U + (u + 1))
                nc.vector.tensor_tensor(Z[:, u, 0:FB], Z[:, u, 0:FB], Z[:, u, 0:FB], ALU.mult).then_inc(sq_ready, 1)

            def save(g, u):
                for c in range(2):
                    dve.wait_ge(pv_done, unit(g, u) * 3 + (1, 3)[c])
                    if not (isinstance(g, int) and unit(g, u) < 2):
                        dve.wait_ge(half_summed, (unit(g, u) - 2) * 2 + (c + 1))
                    nc.vector.tensor_copy(yS[:, (2 * u + c) % 4, :], PS[:, O0 + c, :]).then_inc(o_saved, 1)

            def clamps(g, u, first=False):
                if not first:
                    dve.wait_ge(t_ready, (unit(g, u) - U + 1) * NB)
                for i in range(NP):
                    clamp(g, u, i)

            def normalise(g):
                yt = PS[:, S0, 0:U * NT * VW].rearrange("p (u t w) -> p u t w", u=U, t=NT)
                dve.wait_ge(half_summed, unit(g, U) * 2)
                nc.vector.reciprocal(den[:], yt[:, :, :, D]).then_inc(den_step, 1)
                dve.wait_ge(den_step, 2 * g + 1)
                nc.vector.tensor_tensor(
                    den[:], den[:],
                    spike[:].rearrange("p g t -> p (g t)")[:, bass.ds(g * NT, NT)].unsqueeze(1).to_broadcast([P, U, NT]),
                    ALU.mult).then_inc(den_step, 1)
                dve.wait_ge(den_step, 2 * g + 2)
                yg = Y[:].rearrange("p (b t) (q u d) -> p b q u t d", b=B, q=QUADS, u=U)
                nc.vector.tensor_tensor(
                    yg[:, bass.ds(g // QUADS, 1), bass.ds(g % QUADS, 1), :, :, :].rearrange("p b q u t d -> p (b q u) t d"),
                    yt[:, :, :, 0:D], den[:].unsqueeze(3).to_broadcast([P, U, NT, D]), ALU.mult).then_inc(y_norm, 1)

            def dve_step(g, h, begin=False, first=False, last=False, end=False):
                if begin:
                    clamps(g, 0, first=True)
                if not end:
                    clamps(g, 2 * h + 1, first=first)
                if not begin and not (end and h):
                    square(*prev(g, h)[1])
                if not first:
                    save(*prev2(g, h)[1])
                if not end:
                    add_roots(g, 2 * h)
                    add_roots(g, 2 * h + 1)
                if h and not first:
                    normalise(g - 1)
                if not last:
                    clamps(*after(g, h)[0], first=first and not h)
                if not end:
                    square(g, 2 * h)
                if not begin and not (end and h):
                    save(*prev(g, h)[0])

            dve_step(0, 0, begin=True, first=True)
            dve_step(0, 1, first=True)
            dve_step(1, 0)
            dve_step(1, 1)
            with dve.Fori(2, G - 1) as g:
                dve_step(g, 0)
                dve_step(g, 1)
            dve_step(G - 1, 0)
            dve_step(G - 1, 1, last=True)
            dve_step(G, 0, last=True, end=True)
            dve_step(G, 1, last=True, end=True)

            for n in range(4):
                dve.wait_ge(e_at, n + 1)
                nc.vector.tensor_tensor(x1[:, 4 * n:4 * n + 4, :].rearrange("p t c -> p (t c)"), PS[:, 2 + n, :],
                                        xres[:, 4 * n:4 * n + 4, :].rearrange("p t c -> p (t c)"),
                                        ALU.add).then_inc(e_x1, 1)
            dve.wait_ge(e_x1, 4)
            for t in range(TT):
                last = nc.vector.bn_stats(st6[:, t, :], x1[:, t, :])
            step(last)
            for t in range(TT):
                last = nc.vector.bn_aggr(mv[:, t, :], st6[:, t, :])
            last.then_inc(e_var, 1)
            dve.wait_ge(e_sd, 1)
            step(nc.vector.reciprocal(rstd[:], sd[:]))
            for t in range(TT):
                nc.vector.tensor_scalar(xn2[:, t, :], x1[:, t, :], mv[:, t, 0:1], rstd[:, t:t + 1],
                                        ALU.subtract, ALU.mult).then_inc(e_xn, 1)

            def ffn_out(n):
                dve.wait_ge(e_dn, n + 1)
                nc.vector.tensor_tensor(res[:, n].rearrange("p t c -> p (t c)"), PS[:, 6 + n % 2, :],
                                        x1[:, 4 * n:4 * n + 4, :].rearrange("p t c -> p (t c)"),
                                        ALU.add).then_inc(e_res, 1)

            for n in range(4):
                for a in range(HB):
                    k = n * HB + a
                    dve.wait_ge(e_sil, k + 1)
                    if n >= 2 and a == 0:
                        dve.wait_ge(e_dn, n - 1)
                    nc.vector.tensor_tensor(hT[:, n % 2, a, :], sil[:, k % 2, :], PS[:, 3 + 2 * (k % 2), :],
                                            ALU.mult).then_inc(e_h, 1)
                if n >= 1:
                    ffn_out(n - 1)
            ffn_out(3)

        @block.tensor
        def _(pe):
            mm = nc.tensor.matmul

            def transposes(bank, srcs):
                for i, src in enumerate(srcs):
                    last = nc.tensor.transpose(PS[:, bank, i * P:(i + 1) * P], src, ident[:])
                return last

            pe.wait_ge(consts, 5)
            for n in range(4):
                pe.wait_ge(xn_ready, 4 * n + 4)
                if n >= 2:
                    pe.wait_ge(tr_copied, n - 1)
                transposes(n % 2, [xn[:, 4 * n + i, :] for i in range(4)]).then_inc(tr_ready, 1)
            pe.wait_ge(w_in, 80)
            for t in range(TT):
                pe.wait_ge(tr_copied, t // 4 + 1)
                if t >= 4:
                    pe.wait_ge(qkv_used, t - 3)
                mm(PS[:, QKV_BANKS[t % 4], 0:NW], xnT[:, t * P:(t + 1) * P], W[:], start=True, stop=True
                   ).then_inc(qkv_ready, 1)
            pe.wait_ge(wf_ready, 1)
            for n in range(3):
                pe.wait_ge(tr_copied, n + 3)
                transposes(n % 2, [wf[:, (HB * n + a) * P:(HB * n + a + 1) * P] for a in range(HB)]
                           ).then_inc(tr_ready, 1)
            pe.wait_ge(tr_copied, 7)
            for k in range(8):
                n, s = k // 2, k % 2
                pe.wait_ge(hat_ready, n + 1)
                if k >= 4:
                    pe.wait_ge(r1_ready, k - 3)
                transposes(k % 4, [uq[:, 4 * n + i, s * C:(s + 1) * C] for i in range(4)]).then_inc(hatT_ready, 1)

            def scores(g, u, i, first=False):
                (t, c), e, pr, bank = PIECES[i], ROWS * (u % 2), u // 2, Z0 + i % NZB
                w = min((t + 1) * P - c * BANK, BANK)
                if i == 0:
                    pe.wait_ge(stacks[u], g * NSTK + NSTK)
                if not (first and u * NP + i < NZB):
                    pe.wait_ge(z_used, g * (U * NP) + (u * NP + i + 1 - NZB))
                last = mm(PS[:, bank, 0:w], Qs[e:e + ROWS, pr, t * P:(t + 1) * P],
                          Ks[e:e + ROWS, pr, c * BANK:c * BANK + w], start=True, stop=True)
                if c == t // 4:
                    last = mm(PS[:, bank, w - P:w], identb[:], maskb[:], start=False, stop=True,
                              skip_group_check=True)
                last.then_inc(z_ready, 1)

            def transposed(g, u, k, first=False):
                bank = T0 + k % NTB
                if k == 0:
                    pe.wait_ge(sq_ready, unit(g, u) + 1)
                if not (first and k < NTB):
                    pe.wait_ge(p_ready, unit(g, u) * NB + (k + 1 - NTB))
                o = 0
                for c, jt in BINS[k]:
                    for t in range(max(jt, 4 * c), 4 * c + 4):
                        mm(PS[:, bank, o:o + P], Z[:, u, OFF[t] + jt * P:OFF[t] + (jt + 1) * P], ident[:],
                           is_transpose=True, start=(o == 0), stop=True, skip_group_check=True)
                        o += P
                if k == 0:
                    pe.wait_ge(diag_ready, unit(g, u) + 1)
                o = 0
                for c, jt in BINS[k]:
                    w = width(c, jt)
                    last = mm(PS[:, bank, o:o + w], onesb[:], Dg[:, u % 2, max(jt, 4 * c):4 * c + 4, :],
                              start=False, stop=True, skip_group_check=True)
                    o += w
                last.then_inc(t_ready, 1)

            def values(g, u, lo, hi, first=False):
                for i in range(lo, hi):
                    c, jt = VALUES[i]
                    if i == 0:
                        if u == 0:
                            pe.wait_ge(v_ready, g + 1)
                        pe.wait_ge(p_ready, (unit(g, u) + 1) * NB)
                    if jt == 0 and not first:
                        pe.wait_ge(o_saved, unit(g, u) * 2 - 1 + c)
                    k, o = PLACE[c, jt]
                    w, q = width(c, jt), 32 * (jt % 4)
                    last = mm(PS[q:q + VW, O0 + c, BANK - w:BANK], Vg[:, jt, u, :], PT[:, u % 2, k, o:o + w],
                              start=(jt < 4), stop=True, skip_group_check=True)
                    if jt % 4 == 3:
                        last.then_inc(pv_done, 1)

            def summed(g, u):
                if u == 0:
                    pe.wait_ge(y_norm, g + 1)
                for t in range(NT):
                    if t % 4 == 0:
                        pe.wait_ge(o_saved, unit(g, u) * 2 + (t // 4 + 1))
                    i = u * NT + t
                    last = mm(PS[:, S0, i * VW:(i + 1) * VW], yS[:, (2 * u + t // 4) % 4, (t % 4) * P:(t % 4 + 1) * P],
                              sel[:], start=True, stop=True)
                    if t % 4 == 3:
                        last.then_inc(half_summed, 1)

            def pe_step(g, h, begin=False, first=False, last=False, end=False):
                if begin:
                    for i in range(NP):
                        scores(g, 0, i, first=True)
                for i in range(NP):
                    if not end:
                        scores(g, 2 * h + 1, i, first=begin)
                if not first:
                    values(*prev2(g, h)[1], 0, 12)
                    summed(*prev2(g, h)[0])
                if not begin and not (end and h):
                    for k in range(NTB):
                        transposed(*prev(g, h)[0], k, first=first)
                if not first:
                    summed(*prev2(g, h)[1])
                if not begin and not (end and h):
                    for k in range(NTB, NB):
                        transposed(*prev(g, h)[0], k)
                    for k in range(NTB):
                        transposed(*prev(g, h)[1], k)
                for i in range(NP):
                    if not last:
                        scores(*after(g, h)[0], i)
                    if not begin and not (end and h):
                        values(*prev(g, h)[0], i, i + 1, first=first)
                if not begin and not (end and h):
                    for k in range(NTB, NB):
                        transposed(*prev(g, h)[1], k)

            pe_step(0, 0, begin=True, first=True)
            pe_step(0, 1, first=True)
            with pe.Fori(1, G - 1) as g:
                pe_step(g, 0)
                pe_step(g, 1)
            pe_step(G - 1, 0)
            pe_step(G - 1, 1, last=True)
            pe_step(G, 0, last=True, end=True)
            pe_step(G, 1, last=True, end=True)

            pe.wait_ge(y_norm, G + 1)
            for n in range(4):
                if n >= 2:
                    pe.wait_ge(e_yTc, n - 1)
                transposes(n % 2, [Y[:, 4 * n + i, :] for i in range(4)]
                           ).then_inc(e_yT, 1)
            for n in range(4):
                pe.wait_ge(e_yTc, n + 1)
                for i in range(4):
                    t = 4 * n + i
                    last = mm(PS[:, 2 + n, i * P:(i + 1) * P], yT[:, t * P:(t + 1) * P], Wo[:], start=True, stop=True)
                last.then_inc(e_at, 1)
            for n in range(4):
                pe.wait_ge(e_xn, 4 * n + 4)
                if n >= 2:
                    pe.wait_ge(e_xTc, n - 1)
                transposes(n % 2, [xn2[:, 4 * n + i, :] for i in range(4)]).then_inc(e_xT, 1)

            def down(n):
                pe.wait_ge(e_h, HB * (n + 1))
                if n >= 2:
                    pe.wait_ge(e_res, n - 1)
                for i in range(4):
                    for a in range(HB):
                        last = mm(PS[:, 6 + n % 2, i * P:(i + 1) * P], hT[:, n % 2, a, i * P:(i + 1) * P],
                                  wT[:, 2 * HB + a, :], start=(a == 0), stop=(a == HB - 1))
                last.then_inc(e_dn, 1)

            for n in range(4):
                pe.wait_ge(e_xTc, n + 1)
                for a in range(HB):
                    k = n * HB + a
                    if k >= 2:
                        pe.wait_ge(e_h, k - 1)
                    cols = slice(n * BANK, (n + 1) * BANK)
                    mm(PS[:, 2 + 2 * (k % 2), :], wT[:, a, :], xn2T[:, cols], start=True, stop=True)
                    mm(PS[:, 3 + 2 * (k % 2), :], wT[:, HB + a, :], xn2T[:, cols], start=True, stop=True
                       ).then_inc(e_gu, 1)
                if n >= 1:
                    down(n - 1)
            down(3)


_INS = ['L0_attn_x', 'L0_attn_W_qkv', 'L0_attn_b_qkv', 'L0_attn_W_out', 'L0_attn_b_out', 'L0_attn_w_sur',
        'L0_attn_b_sur', 'L0_attn_threshold', 'L0_ffn_w_gate', 'L0_ffn_w_up', 'L0_ffn_w_down']


def kernel(**inputs):
    import numpy as _np
    import concourse.bacc as _bacc
    from concourse import mybir as _mybir
    from concourse.bass_utils import run_bass_kernel_spmd as _run

    nc = _bacc.Bacc("TRN2", target_bir_lowering=False, num_devices=1)
    arrays, args = {}, []
    for name in _INS:
        a = _np.ascontiguousarray(inputs[name])
        if a.ndim == 0:
            a = a.reshape(1)
        arrays[f"in_{name}"] = a
        args.append(nc.dram_tensor(f"in_{name}", a.shape, _mybir.dt.from_np(a.dtype), kind="ExternalInput").ap())
    args.append(nc.dram_tensor("out_0", (B, T, C), _mybir.dt.float32, kind="ExternalOutput").ap())
    layer(nc, *args)
    r = _run(nc, [arrays], core_ids=[0])
    return r.results[0]["out_0"]
```

```python
import numpy as np
import concourse.bass as bass
from concourse import mybir
from contextlib import ExitStack

fp32 = mybir.dt.float32
bf16 = mybir.dt.bfloat16
i32 = mybir.dt.int32
ALU = mybir.AluOpType
ACT = mybir.ActivationFunctionType
AX = mybir.AxisListType

P = 128
B, T, C, H, HID = 2, 1024, 128, 16, 384
D = C // H
NT = T // P
TT = B * NT
U = 4
G = B * H // U
QUADS = H // U
BANK = 512
OFF = [t * (t + 1) // 2 * P for t in range(NT + 1)]
FU = OFF[NT]
FB = FU + NT
ZW = FB + NT // 2
VW = D + 1
PARTS = 3
ROWS = 64
NZB, NTB = 3, 3
Z0, T0, O0, S0 = 0, NZB, NZB + NTB, NZB + NTB + 1
PIECES = [(t, c) for t in range(NT) for c in range(t // 4 + 1)]
NP = len(PIECES)
BINS = [[(0, 0)], [(0, 1), (0, 3)], [(0, 2), (1, 6)], [(1, 0)], [(1, 1)], [(1, 2)], [(1, 3)], [(1, 4)],
        [(1, 5), (1, 7)]]
NB = len(BINS)


def width(c, jt):
    return (4 * c + 4 - max(jt, 4 * c)) * P


PLACE = {blk: (k, sum(width(*b) for b in bin_[:i])) for k, bin_ in enumerate(BINS) for i, blk in enumerate(bin_)}
VALUES = [(1, j) for j in range(8)] + [(0, j) for j in range(4)]
REPS = (3, 3, 2)
NSTK = 2 * len(REPS) * 16


def unit(g, u):
    return g * U + u


def prev(g, h):
    return [(g, 0), (g, 1)] if h else [(g - 1, 2), (g - 1, 3)]


def prev2(g, h):
    return [(g - 1, 2 * h), (g - 1, 2 * h + 1)]


def after(g, h):
    return [(g + 1, 0), (g + 1, 1)] if h else [(g, 2), (g, 3)]


EXPS = 6
BIN_AFTER = (2, 4, 6)
EPS_LN = 1e-5
ONE_EPS = float(np.float32(1.0 + 1e-7))
MASKED = 1e35
SIGMA = 2.0 ** 0.5
NW = 3 * C + 1
QKV_BANKS = (3, 4, 5, 7)
HB = HID // P
SPLIT_ORDER = [(0, 0), (1, 0), (0, 1), (2, 0), (1, 1), (3, 0), (2, 1), (3, 1)]
YT0, AT0, DN0 = (0, 4), (0, 6), 6
COSH = [1 / 2, 1 / 24, 1 / 720, 1 / 40320, 1 / 3628800]
SINH = [1 / 6, 1 / 120, 1 / 5040, 1 / 362880, 1 / 39916800]


def layer(nc, x, w_qkv, b_qkv, w_out, b_out, w_sur, b_sur, threshold, w_gate, w_up, w_down, out):
    with ExitStack() as ctx:
        def sb(name, shape, dt=fp32):
            return ctx.enter_context(nc.sbuf_tensor(name, shape, dt))

        def sem(name):
            return ctx.enter_context(nc.semaphore(name))

        parts = nc.dram_tensor("qk_parts", [2, B * H, PARTS * D, T], bf16, kind="Internal").ap()

        Z = sb("Z", [P, U, ZW])
        X = sb("X", [P, 2, FB])
        xres = sb("xres", [P, TT, C])
        Y = sb("Y", [P, TT, C])
        V9 = sb("V9", [P, G, NT * U * VW])
        Vg = sb("Vg", [P, NT, U, 2 * VW])
        PT = sb("PT", [P, 2, NB, BANK])
        Qs = sb("Qs", [P, 2, T], bf16)
        Ks = sb("Ks", [P, 2, T], bf16)
        Dg = sb("Dg", [P, 2, NT, P], bf16)
        yS = sb("yS", [P, 2, BANK])
        sel = sb("sel", [P, 2, VW])
        W = sb("W", [P, NW])
        Wb = sb("Wb", [P, NW])
        Wo = sb("Wo", [P, C])
        bo = sb("bo", [P, C])
        thr = sb("thr", [P, 1])
        wT = sb("wT", [P, 3 * HB, P])
        ident = sb("ident", [P, P])
        identb = sb("identb", [P, P], bf16)
        nidentb = sb("nidentb", [P, P], bf16)
        nident = sb("nident", [P, P])
        onesb = sb("onesb", [P, P], bf16)
        maskb = sb("maskb", [P, P], bf16)
        epsln = sb("epsln", [P, 1])
        mhalf = sb("mhalf", [P, 1])
        phalf = sb("phalf", [P, 1])
        st6 = sb("st6", [P, TT, 6])
        mv = sb("mv", [P, TT, 2])
        sd = sb("sd", [P, TT])
        rstd = sb("rstd", [P, TT])
        sur = sb("sur", [P, TT])
        sg = sb("sg", [P, TT])
        spike = sb("spike", [P, G, NT])
        den = sb("den", [P, U, NT])
        PS = ctx.enter_context(nc.psum_tensor("PS", [P, 8, BANK], fp32))

        w2 = NT * 2 * C
        uq = PT[:, 0].rearrange("p k c -> p (k c)")[:, 0:B * w2].rearrange("p (t c) -> p t c", t=TT)
        pt1 = PT[:, 1].rearrange("p k c -> p (k c)")
        usq = pt1[:, 0:B * w2]
        wf = Y[:].rearrange("p t c -> p (t c)")[:, 0:3 * HB * P]
        wint = X[:, 0, 0:3 * HB * P].bitcast(i32).rearrange("p (a d) -> p a d", d=P)
        xn = X[:, 1, 0:TT * C].rearrange("p (t c) -> p t c", t=TT)
        xnT = Z[:, 0, 0:TT * P]
        ws = PARTS * T // 2
        split = [Z[:, 2:4, 0:ws].bitcast(bf16).rearrange("p s (n t) -> p s n t", n=PARTS),
                 pt1[:, 0:2 * ws].rearrange("p (s w) -> p s w", s=2).bitcast(bf16).rearrange(
                     "p s (n t) -> p s n t", n=PARTS)]
        M = NT * 2 * H
        small = [[Z[:, 1, M * i:M * (i + 1)] for i in range(13)],
                 [Z[:, 2 + i // 10, ws + M * (i % 10):ws + M * (i % 10 + 1)] for i in range(13)]]
        names = "mk mc n0 rn n2 ex ei ch sh co p1 p2 cs".split()
        small = [dict(zip(names, tiles)) for tiles in small]
        hw = NT * C
        x1 = xres
        v9f = V9[:].rearrange("p g w -> p (g w)")
        yT = [v9f[:, 0:hw], Z[:, 0, 0:hw]]
        xn2 = [m.rearrange("p (t c) -> p t c", t=NT) for m in (v9f[:, hw:2 * hw], Z[:, 2, 0:hw])]
        xn2T = [v9f[:, 0:hw], Z[:, 1, 0:hw]]
        sil = X[:, 0, 0:2 * BANK].rearrange("p (n t) -> p n t", n=2)
        hT = X[:, 1, 0:2 * HB * BANK].rearrange("p (n a t) -> p n a t", n=2, a=HB)
        res = X[:, 0, 2 * BANK:6 * BANK].rearrange("p (n t c) -> p n t c", n=4, t=4)

        x_in = [sem(f"x_in{n}") for n in range(4)]
        w_in, wo_in, wi_in = sem("w_in"), sem("wo_in"), sem("wi_in")
        consts, wf_ready = sem("consts"), sem("wf_ready")
        dve_s, pool_s, act_s = sem("dve_s"), sem("pool_s"), sem("act_s")
        var_ready, sd_ready, xn_ready, tr_ready, tr_copied = (sem(n) for n in (
            "var_ready", "sd_ready", "xn_ready", "tr_ready", "tr_copied"))
        qkv_ready, qkv_used, usq_ready, mk_ready, root_ready, n2_ready, ex_ready, hat_ready = (sem(n) for n in (
            "qkv_ready", "qkv_used", "usq_ready", "mk_ready", "root_ready", "n2_ready", "ex_ready", "hat_ready"))
        xres_ready, series_ready = sem("xres_ready"), sem("series_ready")
        sg_ready = sem("sg_ready")
        hatT_ready, h1_ready, r1_ready, h2_ready, r2_ready, h3_ready = (sem(n) for n in (
            "hatT_ready", "h1_ready", "r1_ready", "h2_ready", "r2_ready", "h3_ready"))
        stored = [sem(f"stored{b}") for b in range(B)]
        stacks = [sem(f"stacks{u}") for u in range(U)]
        unit_in, y_summed = sem("unit_in"), sem("y_summed")
        z_ready, z_used, roots_ready, sum_ready, log_ready, sq_ready, diag_ready, v_ready = (sem(n) for n in (
            "z_ready", "z_used", "roots_ready", "sum_ready", "log_ready", "sq_ready", "diag_ready", "v_ready"))
        t_ready, p_ready, pv_done, o_saved, den_step, y_norm = (sem(n) for n in (
            "t_ready", "p_ready", "pv_done", "o_saved", "den_step", "y_norm"))
        e_yT, e_yTc, e_at, e_x1, e_var, e_sd, e_xn, e_xT, e_xTc, e_gu, e_sil, e_h, e_dn, e_res, e_out = (
            sem("e_" + n) for n in ("yT", "yTc", "at", "x1", "var", "sd", "xn", "xT", "xTc", "gu", "sil", "h",
                                    "dn", "res", "out"))

        block = ctx.enter_context(nc.Block())

        @block.sync
        def _(sp):
            xt = x.rearrange("b (t p) c -> p (b t) c", p=P)
            for n in range(4):
                sp.dma_start(xres[:, 4 * n:4 * n + 4, :], xt[:, 4 * n:4 * n + 4, :]).then_inc(x_in[n], 16)
            sp.dma_start(wint[:, 0:HB, :], w_gate.rearrange("(a p) d -> p a d", p=P)).then_inc(wi_in, 16)
            sp.dma_start(wint[:, HB:2 * HB, :], w_up.rearrange("(a p) d -> p a d", p=P)).then_inc(wi_in, 16)
            sp.dma_start(wint[:, 2 * HB:3 * HB, :], w_down.rearrange("d (a h) -> d a h", a=HB)).then_inc(wi_in, 16)

            def store_parts(b):
                sp.wait_ge(h3_ready, 4 * (b + 1))
                for s in range(2):
                    for n in range(PARTS):
                        sp.dma_start(parts[s, b * H:(b + 1) * H, n * D:(n + 1) * D, :],
                                     split[b][:, s, n, :]).then_inc(stored[b], 16)

            def load_stacks(n, u):
                r0, pr = ROWS * (u % 2), u // 2
                for i, reps in enumerate(REPS):
                    a, w = r0 + 3 * i * D, reps * D
                    src = parts[0, bass.ds(n, 1), i * D:(i + 1) * D, :].to_broadcast([reps, D, T])
                    sp.dma_start(Qs[a:a + w, pr, :], src).then_inc(stacks[u], 16)
                    src = parts[1, bass.ds(n, 1), 0:w, :].rearrange("o d t -> (o d) t")
                    sp.dma_start(Ks[a:a + w, pr, :], src).then_inc(stacks[u], 16)

            sp.wait_ge(h3_ready, 4)
            for u in range(U):
                r0, pr = ROWS * (u % 2), u // 2
                mine = split[0][u * D:(u + 1) * D]
                for i, reps in enumerate(REPS):
                    a, w = r0 + 3 * i * D, reps * D
                    sp.dma_start(Qs[a:a + w, pr, :], mine[:, 0, i:i + 1, :].to_broadcast([D, reps, T])
                                 ).then_inc(stacks[u], 16)
                    sp.dma_start(Ks[a:a + w, pr, :], mine[:, 1, 0:reps, :]).then_inc(stacks[u], 16)
            for b in range(B):
                store_parts(b)
            for b in range(B):
                sp.wait_ge(stored[b], 16 * 2 * PARTS)
            with sp.Fori(0, G - 1) as g:
                for u in range(U):
                    sp.wait_ge(z_ready, g * (U * NP) + (u + 1) * NP)
                    load_stacks(g * U + (U + u), u)

            ot = out.rearrange("b (t p) c -> p (b t) c", p=P)
            for n in range(4):
                sp.wait_ge(e_res, n + 1)
                sp.dma_start(ot[:, 4 * n:4 * n + 4, :], res[:, n]).then_inc(e_out, 16)
            sp.wait_ge(e_out, 64)

        @block.gpsimd
        def _(pool):
            nc.gpsimd.memset(ident[:], 0.0).then_inc(pool_s, 1)
            nc.gpsimd.memset(maskb[:], 0.0).then_inc(pool_s, 1)
            nc.gpsimd.memset(V9[:], 1.0).then_inc(consts, 1)
            nc.gpsimd.memset(Vg[:], 0.0).then_inc(consts, 1)
            nc.gpsimd.memset(onesb[:], 1.0).then_inc(consts, 1)
            pool.wait_ge(pool_s, 2)
            nc.gpsimd.affine_select(out=ident[:], in_=ident[:], compare_op=ALU.not_equal, fill=1.0, base=0,
                                    pattern=[[-1, P]], channel_multiplier=1).then_inc(pool_s, 1)
            nc.gpsimd.affine_select(out=maskb[:], in_=maskb[:], compare_op=ALU.is_ge, fill=MASKED, base=0,
                                    pattern=[[-1, P]], channel_multiplier=1).then_inc(consts, 1)
            pool.wait_ge(pool_s, 3)
            nc.gpsimd.tensor_copy(identb[:], ident[:]).then_inc(consts, 1)
            nc.gpsimd.tensor_scalar(nident[:], ident[:], -1.0, 0.0, ALU.mult, ALU.add).then_inc(consts, 1)
            nc.gpsimd.tensor_scalar(nidentb[:], ident[:], -1.0, 0.0, ALU.mult, ALU.add).then_inc(consts, 1)
            pool.wait_ge(wi_in, 48)
            nc.gpsimd.tensor_scalar(wf, wint.rearrange("p a d -> p (a d)"),
                                    float(np.float32(1.0 / 127.0)), 0.0, ALU.mult, ALU.add).then_inc(wf_ready, 1)

            pool.wait_ge(qkv_used, TT)

            def pool_group(g, first=False):
                for u in range(U):
                    if u == 2:
                        if not first:
                            pool.wait_ge(pv_done, unit(g, 0))
                        nc.gpsimd.tensor_copy(
                            Vg[:].rearrange("p t u w -> p (t u) w")[:, :, VW:2 * VW],
                            V9[:].rearrange("p g w -> p (g w)")[:, bass.ds(g * (NT * U * VW), NT * U * VW)].rearrange(
                                "p (n w) -> p n w", w=VW)
                        ).then_inc(v_ready, 1)
                    if u >= 2 or not first:
                        pool.wait_ge(t_ready, (unit(g, u) - 1) * NB)
                    pool.wait_ge(sq_ready, unit(g, u) + 1)
                    nc.gpsimd.tensor_tensor(
                        Dg[:, u % 2], nident[:].unsqueeze(1).to_broadcast([P, NT, P]),
                        Z[:, u, FU:FB].unsqueeze(2).to_broadcast([P, NT, P]), ALU.mult).then_inc(diag_ready, 1)

            steps = [3]

            def step(ins):
                steps[0] += 1
                ins.then_inc(pool_s, 1)
                pool.wait_ge(pool_s, steps[0])

            pool.wait_ge(wo_in, 32)
            pool.wait_ge(xn_ready, TT)
            nc.gpsimd.tensor_tensor(xres[:], xres[:], bo[:].unsqueeze(1).to_broadcast([P, TT, C]),
                                    ALU.add).then_inc(xres_ready, 1)
            mc = small[1]["mc"]
            pool.wait_ge(mk_ready, 2)
            step(nc.gpsimd.tensor_scalar(mc, small[1]["mk"], 1.0, None, ALU.min))
            for dst, cf in ((small[1]["p1"], COSH), (small[1]["p2"], SINH)):
                step(nc.gpsimd.tensor_scalar(dst, mc, cf[4], cf[3], ALU.mult, ALU.add))
                for c in (cf[2], cf[1], cf[0]):
                    step(nc.gpsimd.tensor_tensor(dst, dst, mc, ALU.mult))
                    step(nc.gpsimd.tensor_scalar(dst, dst, c, None, ALU.add))
                step(nc.gpsimd.tensor_tensor(dst, dst, mc, ALU.mult))
                nc.gpsimd.tensor_scalar(dst, dst, 1.0, None, ALU.add).then_inc(series_ready, 1)
            pool.wait_ge(consts, 7)
            pool_group(0, first=True)
            with pool.Fori(1, G) as g:
                pool_group(g)

        @block.scalar
        def _(act):
            act.dma_start(W[:, 0:3 * C], w_qkv).then_inc(w_in, 16)
            act.dma_start(W[:, 3 * C:NW], w_sur.unsqueeze(1)).then_inc(w_in, 16)
            act.dma_start(Wb[:, 0:3 * C], b_qkv.partition_broadcast(P)).then_inc(w_in, 16)
            act.dma_start(Wb[:, 3 * C:NW], b_sur.partition_broadcast(P)).then_inc(w_in, 16)
            act.dma_start(thr[:], threshold.partition_broadcast(P)).then_inc(w_in, 16)
            act.dma_start(Wo[:], w_out).then_inc(wo_in, 16)
            act.dma_start(bo[:], b_out.partition_broadcast(P)).then_inc(wo_in, 16)

            act.wait_ge(var_ready, 1)
            nc.scalar.activation(sd[:], mv[:, :, 1], ACT.Sqrt, bias=epsln[:]).then_inc(sd_ready, 1)
            for n in range(4):
                act.wait_ge(tr_ready, n + 1)
                nc.scalar.copy(xnT[:, n * BANK:(n + 1) * BANK], PS[:, n % 2, :]).then_inc(tr_copied, 1)
            def squares(b):
                act.wait_ge(qkv_used, NT * (b + 1))
                nc.scalar.activation(usq[:, b * w2:(b + 1) * w2],
                                     uq[:, b * NT:(b + 1) * NT, :].rearrange("p t c -> p (t c)"),
                                     ACT.Square).then_inc(usq_ready, 1)

            def first_roots(b):
                m = small[b]
                act.wait_ge(mk_ready, b + 1)
                nc.scalar.activation(m["ch"], m["mk"], ACT.Ln).then_inc(act_s, 1)
                act.wait_ge(act_s, b + 1)
                nc.scalar.activation(m["n0"], m["ch"], ACT.Exp, scale=0.5)
                nc.scalar.activation(m["rn"], m["ch"], ACT.Exp, scale=-0.5).then_inc(root_ready, 1)

            def exponentials(b):
                m = small[b]
                act.wait_ge(n2_ready, b + 1)
                nc.scalar.activation(m["ex"], m["n2"], ACT.Exp)
                nc.scalar.activation(m["ei"], m["n2"], ACT.Exp, scale=-1.0).then_inc(ex_ready, 1)

            def split_parts(b):
                for k, part in SPLIT_ORDER:
                    n, s = k // 2, k % 2
                    act.wait_ge((hatT_ready, r1_ready)[part], 4 * b + k + 1)
                    nc.scalar.copy(split[b][:, s, part, n * BANK:(n + 1) * BANK], PS[:, QKV_BANKS[k], :]
                                   ).then_inc((h1_ready, h2_ready)[part], 1)

            nc.scalar.preload_act_table_set("natural_log_exp_and_others")
            squares(0)
            first_roots(0)
            squares(1)
            exponentials(0)
            split_parts(0)
            first_roots(1)
            exponentials(1)
            act.wait_ge(qkv_used, TT)
            nc.scalar.activation(sg[:], sur[:], ACT.Exp, scale=-1.0).then_inc(sg_ready, 1)
            for n in range(3):
                act.wait_ge(tr_ready, n + 5)
                nc.scalar.copy(wT[:, HB * n:HB * (n + 1), :].rearrange("p a d -> p (a d)"),
                               PS[:, n % 2, 0:HID]).then_inc(tr_copied, 1)

            def log(g, u):
                act.wait_ge(sum_ready, unit(g, u) + 1)
                nc.scalar.activation(Z[:, u, 0:FB], Z[:, u, 0:FB], ACT.Ln).then_inc(log_ready, 1)

            def roots(g, u):
                act.wait_ge(unit_in, unit(g, u) + 1)
                nc.scalar.activation(X[:, u % 2, :], Z[:, u, 0:FB], ACT.Sqrt, scale=0.5, bias=mhalf[:])
                nc.scalar.activation(Z[:, u, 0:FB], Z[:, u, 0:FB], ACT.Sqrt, scale=0.5, bias=phalf[:]
                                     ).then_inc(roots_ready, 1)

            def exps(g, u, lo, hi, first=False):
                for k in range(lo, hi):
                    act.wait_ge(t_ready, unit(g, u) * NB + (k + 1))
                    if k == 0 and not first:
                        act.wait_ge(pv_done, unit(g, u) - 1)
                    nc.scalar.activation(PT[:, u % 2, k, :], PS[:, T0 + k % NTB, :], ACT.Exp,
                                         scale=-SIGMA).then_inc(p_ready, 1)

            def copy_yT(b):
                for n in range(2):
                    act.wait_ge(e_yT, 2 * b + n + 1)
                    nc.scalar.copy(yT[b][:, n * BANK:(n + 1) * BANK], PS[:, YT0[b] + n, :]).then_inc(e_yTc, 1)

            def copy_xn2T(b):
                for n in range(2):
                    act.wait_ge(e_xT, 2 * b + n + 1)
                    nc.scalar.copy(xn2T[b][:, n * BANK:(n + 1) * BANK], PS[:, YT0[b] + n, :]).then_inc(e_xTc, 1)

            def silus(lo, hi):
                for k in range(lo, hi):
                    act.wait_ge(e_gu, k + 1)
                    if k >= 2:
                        act.wait_ge(e_h, k - 1)
                    nc.scalar.activation(sil[:, k % 2, :], PS[:, 2 * (k % 2), :], ACT.Silu).then_inc(e_sil, 1)

            def act_step(g, h, begin=False, first=False, last=False, end=False):
                if not end:
                    roots(g, 2 * h)
                    roots(g, 2 * h + 1)
                if last and not end:
                    copy_yT(0)
                if begin:
                    split_parts(1)
                nc.scalar.preload_act_table_set("natural_log_exp_and_others")
                if first:
                    act.wait_ge(stored[1], 16 * 2 * PARTS)
                if not begin:
                    exps(*prev(g, h)[0], 0, EXPS, first=first)
                if not end:
                    log(g, 2 * h)
                if not begin:
                    exps(*prev(g, h)[0], EXPS, NB, first=first)
                if not end:
                    log(g, 2 * h + 1)
                if end:
                    copy_xn2T(0)
                if not begin:
                    exps(*prev(g, h)[1], 0, NB, first=first)
                if last and not end:
                    act.wait_ge(e_var, 1)
                    nc.scalar.activation(sd[:, 0:NT], mv[:, 0:NT, 1], ACT.Ln, bias=epsln[:]).then_inc(act_s, 1)
                    act.wait_ge(act_s, B + 1)
                    nc.scalar.activation(rstd[:, 0:NT], sd[:, 0:NT], ACT.Exp, scale=-0.5).then_inc(e_sd, 1)

            act_step(0, 0, begin=True)
            act_step(0, 1, first=True)
            with act.Fori(1, G - 1) as g:
                act_step(g, 0)
                act_step(g, 1)
            act_step(G - 1, 0)
            act_step(G - 1, 1, last=True)
            act_step(G, 0, last=True, end=True)

            silus(0, 4)
            copy_yT(1)
            silus(4, 6)
            act.wait_ge(e_var, 2)
            nc.scalar.activation(sd[:, NT:TT], mv[:, NT:TT, 1], ACT.Sqrt, bias=epsln[:]).then_inc(e_sd, 1)
            copy_xn2T(1)
            silus(6, 12)

        @block.vector
        def _(dve):
            steps = [0]

            def step(ins):
                steps[0] += 1
                ins.then_inc(dve_s, 1)
                dve.wait_ge(dve_s, steps[0])

            nc.vector.memset(epsln[:], EPS_LN)
            nc.vector.memset(mhalf[:], -0.5)
            nc.vector.memset(phalf[:], 0.5)
            nc.vector.memset(PS[:, O0, :], 0.0).then_inc(y_norm, 1)

            for t in range(TT):
                if t % 4 == 0:
                    dve.wait_ge(x_in[t // 4], 16)
                last = nc.vector.bn_stats(st6[:, t, :], xres[:, t, :])
            step(last)
            for t in range(TT):
                last = nc.vector.bn_aggr(mv[:, t, :], st6[:, t, :])
            last.then_inc(var_ready, 1)
            dve.wait_ge(sd_ready, 1)
            step(nc.vector.reciprocal(rstd[:], sd[:]))
            for t in range(TT):
                last = nc.vector.tensor_scalar(xn[:, t, :], xres[:, t, :], mv[:, t, 0:1], rstd[:, t:t + 1],
                                               ALU.subtract, ALU.mult).then_inc(xn_ready, 1)
            dve.wait_ge(w_in, 80)
            dve.wait_ge(consts, 7)
            for q in range(4):
                nc.vector.tensor_copy(sel[32 * q:32 * q + 32, :, :].rearrange("p c w -> p (c w)"),
                                      ident[32 * q:32 * q + 32, 32 * q:32 * q + 2 * VW])
            v9 = V9[:].rearrange("p (b q) (t u w) -> p b q t u w", b=B, t=NT, u=U)

            def biases(lo, hi):
                for t in range(lo, hi):
                    pq = PS[:, QKV_BANKS[t % 4], :]
                    dve.wait_ge(qkv_ready, t + 1)
                    nc.vector.tensor_tensor(uq[:, t, :], pq[:, 0:2 * C], Wb[:, 0:2 * C], ALU.add)
                    nc.vector.tensor_tensor(v9[:, t // NT, :, t % NT, :, 0:D],
                                            pq[:, 2 * C:3 * C].rearrange("p (q u d) -> p q u d", q=QUADS, u=U),
                                            Wb[:, 2 * C:3 * C].rearrange("p (q u d) -> p q u d", q=QUADS, u=U), ALU.add)
                    nc.vector.tensor_tensor(sur[:, t:t + 1], pq[:, 3 * C:NW], Wb[:, 3 * C:NW],
                                            ALU.add).then_inc(qkv_used, 1)

            def norms(b):
                mk = small[b]["mk"]
                us = usq[:, b * w2:(b + 1) * w2].rearrange("p (m d) -> p m d", d=D)
                dve.wait_ge(usq_ready, b + 1)
                step(nc.vector.tensor_reduce(mk, us[:, :, 1:D], AX.X, ALU.add))
                step(nc.vector.tensor_tensor(mk, mk, us[:, :, 0], ALU.subtract))
                nc.vector.tensor_scalar(mk, mk, 1e-8, None, ALU.max).then_inc(mk_ready, 1)

            def refine(b):
                mk, n0, rn, n2, ch = (small[b][n] for n in ("mk", "n0", "rn", "n2", "ch"))
                dve.wait_ge(mk_ready, b + 1)
                dve.wait_ge(root_ready, b + 1)
                step(nc.vector.tensor_tensor(n2, n0, n0, ALU.mult))
                step(nc.vector.tensor_tensor(n2, mk, n2, ALU.subtract))
                step(nc.vector.scalar_tensor_tensor(n2, n2, 0.5, rn, ALU.mult, ALU.mult))
                nc.vector.tensor_tensor(n2, n2, n0, ALU.add).then_inc(n2_ready, 1)
                dve.wait_ge(n2_ready, b + 1)
                step(nc.vector.tensor_tensor(ch, n2, rn, ALU.mult))
                step(nc.vector.scalar_tensor_tensor(rn, ch, -2.0, rn, ALU.add, ALU.mult))

            def series(b):
                mk, mc, p1, p2 = (small[b][n] for n in ("mk", "mc", "p1", "p2"))
                step(nc.vector.tensor_scalar(mc, mk, 1.0, None, ALU.min))
                for dst, cf in ((p1, COSH), (p2, SINH)):
                    step(nc.vector.tensor_scalar(dst, mc, cf[-1], None, ALU.mult))
                    for c in cf[-2::-1]:
                        step(nc.vector.scalar_tensor_tensor(dst, dst, c, mc, ALU.add, ALU.mult))
                    step(nc.vector.tensor_scalar(dst, dst, 1.0, None, ALU.add))

            def hats(b):
                mk, rn, ex, ei, ch, sh, co, p1, p2, cs = (small[b][n] for n in (
                    "mk", "rn", "ex", "ei", "ch", "sh", "co", "p1", "p2", "cs"))
                dve.wait_ge(ex_ready, b + 1)
                if b:
                    dve.wait_ge(series_ready, 2)
                step(nc.vector.tensor_tensor(sh, ei, ex, ALU.subtract))
                step(nc.vector.scalar_tensor_tensor(co, sh, 0.5, rn, ALU.mult, ALU.mult))
                step(nc.vector.tensor_tensor(ch, ex, ei, ALU.add))
                step(nc.vector.tensor_scalar(cs, ch, 0.5, None, ALU.mult))
                msk = small[b]["mc"].bitcast(i32)
                step(nc.vector.tensor_scalar(msk, mk, 1.0, None, ALU.is_lt))
                step(nc.vector.copy_predicated(co, msk, p2))
                step(nc.vector.copy_predicated(cs, msk, p1))
                coq = co.rearrange("p (t s h) -> p t s h", t=NT, s=2)[:, :, 0, :]
                step(nc.vector.tensor_scalar(coq, coq, -1.0, None, ALU.mult))
                um = uq[:, b * NT:(b + 1) * NT, :].rearrange("p t c -> p (t c)").rearrange("p (m d) -> p m d", d=D)
                for n in range(2):
                    m = slice(P * n, P * (n + 1))
                    nc.vector.tensor_tensor(um[:, m, 1:D], um[:, m, 1:D],
                                            co[:, m].unsqueeze(2).to_broadcast([P, P, D - 1]), ALU.mult)
                    nc.vector.tensor_copy(um[:, m, 0], cs[:, m]).then_inc(hat_ready, 1)

            def last_parts(b):
                for k in range(4):
                    n, s = k // 2, k % 2
                    dve.wait_ge(r2_ready, 4 * b + k + 1)
                    nc.vector.tensor_copy(split[b][:, s, 2, n * BANK:(n + 1) * BANK], PS[:, QKV_BANKS[k], :]
                                          ).then_inc(h3_ready, 1)

            biases(0, NT)
            norms(0)
            biases(NT, NT + 4)
            refine(0)
            biases(NT + 4, TT)
            series(0)
            hats(0)
            norms(1)
            last_parts(0)
            refine(1)

            def clamp(g, u, i):
                t, c = PIECES[i]
                w = min((t + 1) * P - c * BANK, BANK)
                own, col = OFF[t] + c * BANK, FU + t + c * NT // 2
                dve.wait_ge(z_ready, g * (U * NP) + (u * NP + i + 1))
                nc.vector.tensor_scalar(Z[:, u, own:own + w], PS[:, Z0 + i % NZB, 0:w], ONE_EPS, None, ALU.max,
                                        ALU.min, accum_out=Z[:, u, col:col + 1]).then_inc(z_used, 1)
                if i == NP - 1:
                    dve.wait_ge(z_used, g * (U * NP) + (u + 1) * NP)
                    nc.vector.tensor_tensor(Z[:, u, FU + 4:FB], Z[:, u, FU + 4:FB], Z[:, u, FB:ZW],
                                            ALU.min).then_inc(unit_in, 1)

            def add_roots(g, u):
                dve.wait_ge(roots_ready, g * U + (u + 1))
                nc.vector.tensor_tensor(Z[:, u, 0:FB], Z[:, u, 0:FB], X[:, u % 2, :], ALU.add).then_inc(sum_ready, 1)

            def square(g, u):
                dve.wait_ge(log_ready, g * U + (u + 1))
                nc.vector.tensor_tensor(Z[:, u, 0:FB], Z[:, u, 0:FB], Z[:, u, 0:FB], ALU.mult).then_inc(sq_ready, 1)

            def save(g, u):
                dve.wait_ge(pv_done, unit(g, u) + 1)
                if not (isinstance(g, int) and unit(g, u) < 2):
                    dve.wait_ge(y_summed, unit(g, u) - 1)
                nc.vector.tensor_copy(yS[:, u % 2, :], PS[:, O0, :]).then_inc(o_saved, 1)

            def clamps(g, u, first=False):
                if not first:
                    dve.wait_ge(t_ready, (unit(g, u) - U + 1) * NB)
                for i in range(NP):
                    clamp(g, u, i)

            def normalise(g):
                yt = PS[:, S0, 0:U * NT * VW].rearrange("p (u t w) -> p u t w", u=U, t=NT)
                dve.wait_ge(y_summed, unit(g, U))
                nc.vector.reciprocal(den[:], yt[:, :, :, D]).then_inc(den_step, 1)
                dve.wait_ge(den_step, 2 * g + 1)
                nc.vector.tensor_tensor(
                    den[:], den[:],
                    spike[:].rearrange("p g t -> p (g t)")[:, bass.ds(g * NT, NT)].unsqueeze(1).to_broadcast([P, U, NT]),
                    ALU.mult).then_inc(den_step, 1)
                dve.wait_ge(den_step, 2 * g + 2)
                yg = Y[:].rearrange("p (b t) (q u d) -> p b q u t d", b=B, q=QUADS, u=U)
                nc.vector.tensor_tensor(
                    yg[:, bass.ds(g // QUADS, 1), bass.ds(g % QUADS, 1), :, :, :].rearrange("p b q u t d -> p (b q u) t d"),
                    yt[:, :, :, 0:D], den[:].unsqueeze(3).to_broadcast([P, U, NT, D]), ALU.mult).then_inc(y_norm, 1)

            def spikes():
                dve.wait_ge(sg_ready, 1)
                step(nc.vector.tensor_scalar(sg[:], sg[:], 1.0, None, ALU.add))
                step(nc.vector.reciprocal(sg[:], sg[:]))
                for b in range(B):
                    step(nc.vector.tensor_scalar(
                        spike[:, b * QUADS:(b + 1) * QUADS, :],
                        sg[:, b * NT:(b + 1) * NT].unsqueeze(1).to_broadcast([P, QUADS, NT]),
                        thr[:], None, ALU.is_gt))

            def residual(b):
                for n in range(2 * b, 2 * b + 2):
                    dve.wait_ge(e_at, n + 1)
                    dve.wait_ge(xres_ready, 1)
                    xc = xres[:, 4 * n:4 * n + 4, :].rearrange("p t c -> p (t c)")
                    nc.vector.tensor_tensor(xc, PS[:, AT0[b] + n % 2, :], xc, ALU.add).then_inc(e_x1, 1)
                dve.wait_ge(e_x1, 2 * b + 2)

            def statistics(b):
                for t in range(b * NT, (b + 1) * NT):
                    last = nc.vector.bn_stats(st6[:, t, :], x1[:, t, :])
                step(last)
                for t in range(b * NT, (b + 1) * NT):
                    last = nc.vector.bn_aggr(mv[:, t, :], st6[:, t, :])
                last.then_inc(e_var, 1)
                dve.wait_ge(e_var, b + 1)

            def standardise(b):
                dve.wait_ge(e_sd, b + 1)
                for t in range(NT):
                    i = b * NT + t
                    nc.vector.tensor_scalar(xn2[b][:, t, :], x1[:, i, :], mv[:, i, 0:1], rstd[:, i:i + 1],
                                            ALU.subtract, ALU.mult).then_inc(e_xn, 1)

            def gated(lo, hi):
                for k in range(lo, hi):
                    n, a = k // HB, k % HB
                    dve.wait_ge(e_sil, k + 1)
                    if n >= 2 and a == 0:
                        dve.wait_ge(e_dn, n - 1)
                    nc.vector.tensor_tensor(hT[:, n % 2, a, :], sil[:, k % 2, :], PS[:, 2 * (k % 2) + 1, :],
                                            ALU.mult).then_inc(e_h, 1)

            def ffn_out(n):
                dve.wait_ge(e_dn, n + 1)
                nc.vector.tensor_tensor(res[:, n].rearrange("p t c -> p (t c)"), PS[:, DN0 + n % 2, :],
                                        x1[:, 4 * n:4 * n + 4, :].rearrange("p t c -> p (t c)"),
                                        ALU.add).then_inc(e_res, 1)

            def dve_step(g, h, begin=False, first=False, last=False, end=False):
                if begin:
                    clamps(g, 0, first=True)
                if not end:
                    clamps(g, 2 * h + 1, first=first)
                if begin:
                    hats(1)
                else:
                    square(*prev(g, h)[1])
                if end:
                    dve.wait_ge(v_ready, G)
                    standardise(0)
                if not first:
                    save(*prev2(g, h)[0])
                if not end:
                    add_roots(g, 2 * h)
                if not first:
                    save(*prev2(g, h)[1])
                if not end:
                    add_roots(g, 2 * h + 1)
                if begin:
                    last_parts(1)
                    spikes()
                    dve.wait_ge(stored[0], 16 * 2 * PARTS)
                    for u in range(U):
                        dve.wait_ge(stacks[u], NSTK)
                if h and not first:
                    normalise(g - 1)
                if last and not end:
                    residual(0)
                    statistics(0)
                if not last:
                    clamps(*after(g, h)[0], first=first and not h)
                if not end:
                    square(g, 2 * h)
                if end:
                    save(*prev(g, h)[0])

            dve_step(0, 0, begin=True, first=True)
            dve_step(0, 1, first=True)
            dve_step(1, 0)
            dve_step(1, 1)
            with dve.Fori(2, G - 1) as g:
                dve_step(g, 0)
                dve_step(g, 1)
            dve_step(G - 1, 0)
            dve_step(G - 1, 1, last=True)
            dve_step(G, 0, last=True, end=True)

            gated(0, 1)
            save(G - 1, 3)
            gated(1, 3)
            normalise(G - 1)
            gated(3, 5)
            residual(1)
            statistics(1)
            gated(5, 6)
            dve.wait_ge(e_sd, 2)
            step(nc.vector.reciprocal(rstd[:, NT:TT], sd[:, NT:TT]))
            standardise(1)
            ffn_out(0)
            ffn_out(1)
            gated(6, 12)
            ffn_out(2)
            ffn_out(3)

        @block.tensor
        def _(pe):
            mm = nc.tensor.matmul

            def transposes(bank, srcs):
                for i, src in enumerate(srcs):
                    last = mm(PS[:, bank, i * P:(i + 1) * P], src, ident[:], is_transpose=True, start=(i == 0), stop=True,
                              skip_group_check=True)
                return last

            pe.wait_ge(consts, 7)
            for n in range(4):
                pe.wait_ge(xn_ready, 4 * n + 4)
                if n >= 2:
                    pe.wait_ge(tr_copied, n - 1)
                transposes(n % 2, [xn[:, 4 * n + i, :] for i in range(4)]).then_inc(tr_ready, 1)
            pe.wait_ge(w_in, 80)
            for t in range(TT):
                pe.wait_ge(tr_copied, t // 4 + 1)
                if t >= 4:
                    pe.wait_ge(qkv_used, t - 3)
                mm(PS[:, QKV_BANKS[t % 4], 0:NW], xnT[:, t * P:(t + 1) * P], W[:], start=True, stop=True
                   ).then_inc(qkv_ready, 1)

            def split_rests(b):
                for k in range(4):
                    n, s = k // 2, k % 2
                    pe.wait_ge(hat_ready, 2 * b + n + 1)
                    if b:
                        pe.wait_ge(h3_ready, k + 1)
                    transposes(QKV_BANKS[k], [uq[:, NT * b + 4 * n + i, s * C:(s + 1) * C] for i in range(4)]
                               ).then_inc(hatT_ready, 1)
                for k, part in SPLIT_ORDER:
                    n, s = k // 2, k % 2
                    pe.wait_ge((h1_ready, h2_ready)[part], 4 * b + k + 1)
                    mm(PS[:, QKV_BANKS[k], :], nidentb[:], split[b][:, s, part, n * BANK:(n + 1) * BANK],
                       start=False, stop=True, skip_group_check=True).then_inc((r1_ready, r2_ready)[part], 1)

            split_rests(0)
            pe.wait_ge(wf_ready, 1)
            for n in range(3):
                pe.wait_ge(tr_copied, n + 3)
                transposes(n % 2, [wf[:, (HB * n + a) * P:(HB * n + a + 1) * P] for a in range(HB)]
                           ).then_inc(tr_ready, 1)
            pe.wait_ge(tr_copied, 7)

            def scores(g, u, i, first=False):
                (t, c), e, pr, bank = PIECES[i], ROWS * (u % 2), u // 2, Z0 + i % NZB
                w = min((t + 1) * P - c * BANK, BANK)
                if i == 0:
                    pe.wait_ge(stacks[u], g * NSTK + NSTK)
                if not (first and u * NP + i < NZB):
                    pe.wait_ge(z_used, g * (U * NP) + (u * NP + i + 1 - NZB))
                last = mm(PS[:, bank, 0:w], Qs[e:e + ROWS, pr, t * P:(t + 1) * P],
                          Ks[e:e + ROWS, pr, c * BANK:c * BANK + w], start=True, stop=True)
                if c == t // 4:
                    last = mm(PS[:, bank, w - P:w], identb[:], maskb[:], start=False, stop=True,
                              skip_group_check=True)
                last.then_inc(z_ready, 1)

            def transposed(g, u, k, first=False):
                bank = T0 + k % NTB
                if k == 0:
                    pe.wait_ge(sq_ready, unit(g, u) + 1)
                if not (first and k < NTB):
                    pe.wait_ge(p_ready, unit(g, u) * NB + (k + 1 - NTB))
                o = 0
                for c, jt in BINS[k]:
                    for t in range(max(jt, 4 * c), 4 * c + 4):
                        mm(PS[:, bank, o:o + P], Z[:, u, OFF[t] + jt * P:OFF[t] + (jt + 1) * P], ident[:],
                           is_transpose=True, start=(o == 0), stop=True, skip_group_check=True)
                        o += P
                if k == 0:
                    pe.wait_ge(diag_ready, unit(g, u) + 1)
                o = 0
                for c, jt in BINS[k]:
                    w = width(c, jt)
                    last = mm(PS[:, bank, o:o + w], onesb[:], Dg[:, u % 2, max(jt, 4 * c):4 * c + 4, :],
                              start=False, stop=True, skip_group_check=True)
                    o += w
                last.then_inc(t_ready, 1)

            def values(g, u):
                if u == 0:
                    pe.wait_ge(v_ready, g + 1)
                pe.wait_ge(p_ready, (unit(g, u) + 1) * NB)
                if not (isinstance(g, int) and unit(g, u) == 0):
                    pe.wait_ge(o_saved, unit(g, u))
                for i, (c, jt) in enumerate(VALUES):
                    k, o = PLACE[c, jt]
                    w, q = width(c, jt), 32 * (jt % 4)
                    v = Vg[:, jt, u, (1 - c) * VW:2 * VW]
                    last = mm(PS[q:q + (1 + c) * VW, O0, BANK - w:BANK], v, PT[:, u % 2, k, o:o + w],
                              start=(i < 4), stop=True, skip_group_check=True)
                last.then_inc(pv_done, 1)

            def summed(g, u):
                if u == 0:
                    pe.wait_ge(y_norm, g + 1)
                pe.wait_ge(o_saved, unit(g, u) + 1)
                yt = PS[:, S0, u * NT * VW:(u + 1) * NT * VW].rearrange("p (c i w) -> p c i w", c=2, w=VW)
                for i in range(4):
                    last = mm(yt[:, :, i, :], yS[:, u % 2, i * P:(i + 1) * P], sel[:], start=True, stop=True)
                last.then_inc(y_summed, 1)

            def y_transposes(b):
                pe.wait_ge(y_norm, QUADS * (b + 1) + 1)
                pe.wait_ge(z_used, G * U * NP)
                for n in range(2):
                    transposes(YT0[b] + n, [Y[:, NT * b + 4 * n + i, :] for i in range(4)]).then_inc(e_yT, 1)

            def out_projection(b):
                for n in range(2):
                    pe.wait_ge(e_yTc, 2 * b + n + 1)
                    for i in range(4):
                        t = 4 * n + i
                        last = mm(PS[:, AT0[b] + n, i * P:(i + 1) * P], yT[b][:, t * P:(t + 1) * P], Wo[:],
                                  start=True, stop=True)
                    last.then_inc(e_at, 1)

            def x_transposes(b):
                pe.wait_ge(e_xn, NT * (b + 1))
                for n in range(2):
                    transposes(YT0[b] + n, [xn2[b][:, 4 * n + i, :] for i in range(4)]).then_inc(e_xT, 1)

            def gate_up(k):
                n, a = k // HB, k % HB
                pe.wait_ge(e_xTc, n + 1)
                if k >= 2:
                    pe.wait_ge(e_h, k - 1)
                cols = xn2T[n // 2][:, (n % 2) * BANK:(n % 2 + 1) * BANK]
                mm(PS[:, 2 * (k % 2), :], wT[:, a, :], cols, start=True, stop=True)
                mm(PS[:, 2 * (k % 2) + 1, :], wT[:, HB + a, :], cols, start=True, stop=True).then_inc(e_gu, 1)

            def down(n):
                pe.wait_ge(e_h, HB * (n + 1))
                if n == 0:
                    pe.wait_ge(e_x1, 4)
                if n >= 2:
                    pe.wait_ge(e_res, n - 1)
                for i in range(4):
                    for a in range(HB):
                        last = mm(PS[:, DN0 + n % 2, i * P:(i + 1) * P], hT[:, n % 2, a, i * P:(i + 1) * P],
                                  wT[:, 2 * HB + a, :], start=(a == 0), stop=(a == HB - 1))
                last.then_inc(e_dn, 1)

            def pe_step(g, h, begin=False, first=False, last=False, end=False):
                if begin:
                    for i in range(NP):
                        scores(g, 0, i, first=True)
                if not end:
                    for i in range(NP):
                        scores(g, 2 * h + 1, i, first=begin)
                if begin:
                    split_rests(1)
                if not first:
                    values(*prev2(g, h)[0])
                    values(*prev2(g, h)[1])
                    summed(*prev2(g, h)[0])
                if not begin:
                    for k in range(NTB):
                        transposed(*prev(g, h)[0], k, first=first)
                if end:
                    x_transposes(0)
                elif last:
                    y_transposes(0)
                if not begin:
                    for k in range(NTB, NB):
                        transposed(*prev(g, h)[0], k)
                if not first:
                    summed(*prev2(g, h)[1])
                if last and not end:
                    out_projection(0)
                for i in range(NP):
                    if not last:
                        scores(*after(g, h)[0], i)
                    if not begin and i in BIN_AFTER:
                        transposed(*prev(g, h)[1], BIN_AFTER.index(i))
                if end:
                    values(*prev(g, h)[0])
                if not begin:
                    for k in range(len(BIN_AFTER), NB):
                        transposed(*prev(g, h)[1], k)

            pe_step(0, 0, begin=True, first=True)
            pe_step(0, 1, first=True)
            pe_step(1, 0)
            pe_step(1, 1)
            with pe.Fori(2, G - 1) as g:
                pe_step(g, 0)
                pe_step(g, 1)
            pe_step(G - 1, 0)
            pe_step(G - 1, 1, last=True)
            pe_step(G, 0, last=True, end=True)

            gate_up(0)
            values(G - 1, 3)
            gate_up(1)
            summed(G - 1, 2)
            gate_up(2)
            summed(G - 1, 3)
            gate_up(3)
            y_transposes(1)
            gate_up(4)
            out_projection(1)
            gate_up(5)
            down(0)
            down(1)
            x_transposes(1)
            for k in range(6, 10):
                gate_up(k)
            down(2)
            for k in range(10, 12):
                gate_up(k)
            down(3)


_INS = ['L0_attn_x', 'L0_attn_W_qkv', 'L0_attn_b_qkv', 'L0_attn_W_out', 'L0_attn_b_out', 'L0_attn_w_sur',
        'L0_attn_b_sur', 'L0_attn_threshold', 'L0_ffn_w_gate', 'L0_ffn_w_up', 'L0_ffn_w_down']


def kernel(**inputs):
    import numpy as _np
    import concourse.bacc as _bacc
    from concourse import mybir as _mybir
    from concourse.bass_utils import run_bass_kernel_spmd as _run

    nc = _bacc.Bacc("TRN2", target_bir_lowering=False, num_devices=1)
    arrays, args = {}, []
    for name in _INS:
        a = _np.ascontiguousarray(inputs[name])
        if a.ndim == 0:
            a = a.reshape(1)
        arrays[f"in_{name}"] = a
        args.append(nc.dram_tensor(f"in_{name}", a.shape, _mybir.dt.from_np(a.dtype), kind="ExternalInput").ap())
    args.append(nc.dram_tensor("out_0", (B, T, C), _mybir.dt.float32, kind="ExternalOutput").ap())
    layer(nc, *args)
    r = _run(nc, [arrays], core_ids=[0])
    return r.results[0]["out_0"]
```
